# Optimizing a Trainium2 kernel written in Bass

```python
import numpy as np
import jax
import jax.numpy as jnp

def _softmax(x, axis=-1):
    return jax.nn.softmax(x, axis=axis)

def _gelu(x):
    return jax.nn.gelu(x, approximate=True)

def _silu(x):
    return jax.nn.silu(x)

def _sigmoid(x):
    return jax.nn.sigmoid(x)

def _layernorm(x, axis=-1, eps=1e-05):
    m = jnp.mean(x, axis=axis, keepdims=True)
    v = jnp.var(x, axis=axis, keepdims=True)
    return (x - m) / jnp.sqrt(v + eps)

def _scatter_add(tgt, idx, src, axis=0):
    return tgt.at[idx].add(src)

def _segment_sum(src, seg, n):
    return jax.ops.segment_sum(src, seg, n)
kernel_name = 'mk_gps_d4_gnn_r8_0fbc34'

def setup_inputs(seed: int=0):
    np.random.seed(seed)
    _w = jnp.asarray

    def _rec_inputs():
        import jax
        import jax.numpy as jnp
        _gk = jax.random.key(seed)
        x = -0.0002117 + 1 * jax.random.normal(jax.random.fold_in(_gk, 1), (1250, 512), jnp.float32)
        src = jax.random.randint(jax.random.fold_in(_gk, 2), (20000,), 0, 1250, jnp.int32)
        dst = jnp.minimum((1250 * jax.random.uniform(jax.random.fold_in(_gk, 3), (20000,)) ** 2.0).astype(jnp.int32), 9999)
        _o = jnp.argsort(dst, stable=True)
        src = src[_o]
        dst = dst[_o]
        return (x, src, dst)
    x, src, dst = _rec_inputs()

    def _L0_gnn_setup():
        import jax, jax.numpy as jnp
        import numpy as np
        N_NODES = 6250
        N_EDGES = 50000
        IN_DIM = 512
        OUT_DIM = 512
        key = jax.random.key(seed)
        k1, k2, k3, k4 = jax.random.split(key, 4)
        x = jax.random.normal(k1, (N_NODES, IN_DIM), dtype=jnp.float32)
        edge_index = jax.random.randint(k2, (2, N_EDGES), 0, N_NODES, dtype=jnp.int64)
        W = jax.random.normal(k3, (OUT_DIM, IN_DIM), dtype=jnp.float32) / np.sqrt(IN_DIM)
        b = jax.random.normal(k4, (OUT_DIM,), dtype=jnp.float32) * 0.01
        return {'x': x, 'edge_index': edge_index, 'W': W, 'b': b}
    _L0_gnn_all = _L0_gnn_setup()
    _L0_gnn_in = {k: v for k, v in _L0_gnn_all.items() if k in ('W', 'b')}
    del _L0_gnn_all

    def _L0_mix_setup():
        import jax, jax.numpy as jnp
        import numpy as np
        DEPTH, DIM, HEADS, DIM_HEAD, NBF, MULT = (2, 512, 8, 64, 256, 4)
        INNER = HEADS * DIM_HEAD

        def layernorm(x, g, b, eps=1e-05):
            mu = jnp.mean(x, axis=-1, keepdims=True)
            var = jnp.mean((x - mu) ** 2, axis=-1, keepdims=True)
            return (x - mu) * jax.lax.rsqrt(var + eps) * g + b

        def softmax_kernel(data, proj, is_query, eps=0.0001):
            d = data.shape[-1]
            normalizer = d ** (-0.25)
            ratio = proj.shape[0] ** (-0.5)
            data_dash = jnp.einsum('bhnd,md->bhnm', data * normalizer, proj)
            diag = jnp.sum(data ** 2, axis=-1, keepdims=True) * 0.5 * normalizer ** 2
            if is_query:
                m = jnp.max(data_dash, axis=-1, keepdims=True)
            else:
                m = jnp.max(data_dash, axis=(-2, -1), keepdims=True)
            m = jax.lax.stop_gradient(m)
            return ratio * (jnp.exp(data_dash - diag - m) + eps)
        key = jax.random.key(seed)
        ks = jax.random.split(key, 16)
        s = 0.02
        B, N = (4, 1024)
        inp = {'x': jax.random.normal(ks[0], (B, N, DIM), jnp.float32), 'ln1_g': jnp.ones((DEPTH, DIM), jnp.float32), 'ln1_b': jnp.zeros((DEPTH, DIM), jnp.float32), 'ln2_g': jnp.ones((DEPTH, DIM), jnp.float32), 'ln2_b': jnp.zeros((DEPTH, DIM), jnp.float32), 'Wq': jax.random.normal(ks[1], (DEPTH, DIM, INNER), jnp.float32) * s, 'bq': jnp.zeros((DEPTH, INNER), jnp.float32), 'Wk': jax.random.normal(ks[2], (DEPTH, DIM, INNER), jnp.float32) * s, 'bk': jnp.zeros((DEPTH, INNER), jnp.float32), 'Wv': jax.random.normal(ks[3], (DEPTH, DIM, INNER), jnp.float32) * s, 'bv': jnp.zeros((DEPTH, INNER), jnp.float32), 'Wo': jax.random.normal(ks[4], (DEPTH, INNER, DIM), jnp.float32) * s, 'bo': jnp.zeros((DEPTH, DIM), jnp.float32), 'proj': jax.random.normal(ks[5], (DEPTH, NBF, DIM_HEAD), jnp.float32), 'W1': jax.random.normal(ks[6], (DEPTH, DIM, DIM * MULT), jnp.float32) * s, 'b1': jnp.zeros((DEPTH, DIM * MULT), jnp.float32), 'W2': jax.random.normal(ks[7], (DEPTH, DIM * MULT, DIM), jnp.float32) * s, 'b2': jnp.zeros((DEPTH, DIM), jnp.float32)}
        return inp
    _L0_mix_all = _L0_mix_setup()
    _L0_mix_in = {k: v for k, v in _L0_mix_all.items() if k in ('ln1_g', 'ln1_b', 'ln2_g', 'ln2_b', 'Wq', 'bq', 'Wk', 'bk', 'Wv', 'bv', 'Wo', 'bo', 'proj', 'W1', 'b1', 'W2', 'b2')}
    del _L0_mix_all

    def _L0_ffn_setup():
        import jax, jax.numpy as jnp
        import numpy as np
        B, S, H, E, K, DF, SH = (8, 512, 512, 8, 2, 128, 512)
        key = jax.random.key(seed)
        ks = jax.random.split(key, 10)
        n = lambda i, shape, sc: jax.random.normal(ks[i], shape, jnp.float32) * sc
        return {'hidden_states': n(0, (B, S, H), 1.0), 'gate_w': n(1, (E, H), 0.05), 'w1': n(2, (E, H, DF), 0.05), 'b1': n(3, (E, DF), 0.01), 'w2': n(4, (E, DF, H), 0.05), 'b2': n(5, (E, H), 0.01), 'sw1': n(6, (H, SH), 0.05), 'sb1': n(7, (SH,), 0.01), 'sw2': n(8, (SH, H), 0.05), 'sb2': n(9, (H,), 0.01)}
    _L0_ffn_all = _L0_ffn_setup()
    _L0_ffn_in = {k: v for k, v in _L0_ffn_all.items() if k in ('gate_w', 'w1', 'b1', 'w2', 'b2', 'sw1', 'sb1', 'sw2', 'sb2')}
    del _L0_ffn_all

    def _L1_gnn_setup():
        import jax, jax.numpy as jnp
        import numpy as np
        N, E, D = (6250, 50000, 512)
        EPS = 1e-05
        key = jax.random.key(seed)
        ks = jax.random.split(key, 5)
        scale = 1.0 / np.sqrt(D)
        x = jax.random.normal(ks[0], (N, D), dtype=jnp.float32)
        edge_index = jax.random.randint(ks[1], (2, E), 0, N, dtype=jnp.int32)
        W_l = jax.random.normal(ks[2], (D, D), dtype=jnp.float32) * scale
        b_l = jnp.zeros((D,), dtype=jnp.float32)
        W_r = jax.random.normal(ks[3], (D, D), dtype=jnp.float32) * scale
        gamma = jnp.ones((D,), dtype=jnp.float32)
        beta = jnp.zeros((D,), dtype=jnp.float32)
        return {'x': x, 'edge_index': edge_index, 'W_l': W_l, 'b_l': b_l, 'W_r': W_r, 'gamma': gamma, 'beta': beta}
    _L1_gnn_all = _L1_gnn_setup()
    _L1_gnn_in = {k: v for k, v in _L1_gnn_all.items() if k in ('W_l', 'b_l', 'W_r', 'gamma', 'beta')}
    del _L1_gnn_all

    def _L1_mix_setup():
        import jax, jax.numpy as jnp
        import numpy as np
        DIM = 512
        H = 8
        C = 64
        HID = H * C
        NMEM = H

        def _rmsnorm_seq(x, w):
            n = jnp.sqrt(jnp.sum(x * x, axis=2, keepdims=True))
            return x / jnp.maximum(n, 1e-12) * w * jnp.asarray(DIM ** 0.5, x.dtype)
        key = jax.random.key(seed)
        ks = jax.random.split(key, 7)
        b, n = (4, 512)
        x = jax.random.normal(ks[0], (b, n, DIM), dtype=jnp.float32)
        norm_w = jnp.ones((1, 1, DIM), dtype=jnp.float32)
        w_qkv = jax.random.normal(ks[1], (DIM, 3 * HID), dtype=jnp.float32) / np.sqrt(DIM)
        mem_kv = jax.random.normal(ks[2], (2, H, C, NMEM), dtype=jnp.float32)
        w_out = jax.random.normal(ks[3], (HID, DIM), dtype=jnp.float32) / np.sqrt(HID)
        b_out = jax.random.normal(ks[4], (DIM,), dtype=jnp.float32) * 0.01
        out_norm_w = jnp.ones((1, 1, DIM), dtype=jnp.float32)
        return {'x': x, 'norm_w': norm_w, 'w_qkv': w_qkv, 'mem_kv': mem_kv, 'w_out': w_out, 'b_out': b_out, 'out_norm_w': out_norm_w}
    _L1_mix_all = _L1_mix_setup()
    _L1_mix_in = {k: v for k, v in _L1_mix_all.items() if k in ('norm_w', 'w_qkv', 'mem_kv', 'w_out', 'b_out', 'out_norm_w')}
    del _L1_mix_all

    def _L1_ffn_setup():
        import jax, jax.numpy as jnp
        import numpy as np
        E = 8
        TOP_K = 2
        D = 512
        H = 1024
        B, S = (16, 512)
        key = jax.random.key(seed)
        ks = jax.random.split(key, 10)
        sd = lambda fan_in: 1.0 / np.sqrt(fan_in)
        x = jax.random.normal(ks[0], (B, S, D), dtype=jnp.float32)
        gw1 = jax.random.uniform(ks[1], (D, D // 2), jnp.float32, -sd(D), sd(D))
        gb1 = jnp.zeros((D // 2,), jnp.float32)
        gw2 = jax.random.uniform(ks[2], (D // 2, E), jnp.float32, -sd(D // 2), sd(D // 2))
        gb2 = jnp.zeros((E,), jnp.float32)
        we1 = jax.random.uniform(ks[3], (E, D, H), jnp.float32, -sd(D), sd(D))
        be1 = jnp.zeros((E, H), jnp.float32)
        we2 = jax.random.uniform(ks[4], (E, H, D), jnp.float32, -sd(H), sd(H))
        be2 = jnp.zeros((E, D), jnp.float32)
        return {'x': x, 'gw1': gw1, 'gb1': gb1, 'gw2': gw2, 'gb2': gb2, 'we1': we1, 'be1': be1, 'we2': we2, 'be2': be2}
    _L1_ffn_all = _L1_ffn_setup()
    _L1_ffn_in = {k: v for k, v in _L1_ffn_all.items() if k in ('gw1', 'gb1', 'gw2', 'gb2', 'we1', 'be1', 'we2', 'be2')}
    del _L1_ffn_all

    def _L2_gnn_setup():
        import jax, jax.numpy as jnp
        import numpy as np
        N_NODES = 1250
        N_EDGES = 20000
        D = 512
        key = jax.random.key(seed)
        k_h, k_e, k_w1, k_w2 = jax.random.split(key, 4)
        h = jax.random.normal(k_h, (N_NODES, D), dtype=jnp.float32)
        edge_index = jax.random.randint(k_e, (2, N_EDGES), 0, N_NODES, dtype=jnp.int64)
        scale = 1.0 / np.sqrt(D)
        W1 = jax.random.normal(k_w1, (D, D), dtype=jnp.float32) * scale
        b1 = jnp.zeros((D,), dtype=jnp.float32)
        W2 = jax.random.normal(k_w2, (D, D), dtype=jnp.float32) * scale
        b2 = jnp.zeros((D,), dtype=jnp.float32)
        return {'h': h, 'edge_index': edge_index, 'W1': W1, 'b1': b1, 'W2': W2, 'b2': b2}
    _L2_gnn_all = _L2_gnn_setup()
    _L2_gnn_in = {k: v for k, v in _L2_gnn_all.items() if k in ('W1', 'b1', 'W2', 'b2')}
    del _L2_gnn_all

    def _L2_mix_setup():
        import jax, jax.numpy as jnp
        import numpy as np
        HEADS = 8
        DIM_HEAD = 64
        key = jax.random.key(seed)
        k1, k2, k3 = jax.random.split(key, 3)
        B, L, D = (8, 512, 512)
        hidden = HEADS * DIM_HEAD
        x = jax.random.normal(k1, (B, L, D), dtype=jnp.float32)
        Wqkv = jax.random.normal(k2, (3 * hidden, D), dtype=jnp.float32) * (1.0 / np.sqrt(D))
        Wout = jax.random.normal(k3, (D, hidden), dtype=jnp.float32) * (1.0 / np.sqrt(hidden))
        bout = jnp.zeros((D,), dtype=jnp.float32)
        return {'x': x, 'Wqkv': Wqkv, 'Wout': Wout, 'bout': bout}
    _L2_mix_all = _L2_mix_setup()
    _L2_mix_in = {k: v for k, v in _L2_mix_all.items() if k in ('Wqkv', 'Wout', 'bout')}
    del _L2_mix_all

    def _L2_ffn_setup():
        import jax, jax.numpy as jnp
        import numpy as np
        E = 8
        K = 2
        D = 512
        H = 256
        EPS = 1e-06

        def _rmsnorm(x, w):
            return x * jax.lax.rsqrt(jnp.mean(x * x, axis=-1, keepdims=True) + EPS) * w
        key = jax.random.key(seed)
        ks = jax.random.split(key, 5)
        B, T = (4, 256)
        x = jax.random.normal(ks[0], (B, T, D), dtype=jnp.float32)
        gate_w = jax.random.normal(ks[1], (D, E), dtype=jnp.float32) / np.sqrt(D)
        w1 = jax.random.normal(ks[2], (E, D, H), dtype=jnp.float32) / np.sqrt(D)
        w2 = jax.random.normal(ks[3], (E, H, H), dtype=jnp.float32) / np.sqrt(H)
        w3 = jax.random.normal(ks[4], (E, H, D), dtype=jnp.float32) / np.sqrt(H)
        n1 = jnp.ones((E, H), dtype=jnp.float32)
        n2 = jnp.ones((E, H), dtype=jnp.float32)
        return {'x': x, 'gate_w': gate_w, 'w1': w1, 'w2': w2, 'w3': w3, 'n1': n1, 'n2': n2}
    _L2_ffn_all = _L2_ffn_setup()
    _L2_ffn_in = {k: v for k, v in _L2_ffn_all.items() if k in ('gate_w', 'w1', 'w2', 'w3', 'n1', 'n2')}
    del _L2_ffn_all

    def _L3_gnn_setup():
        import jax, jax.numpy as jnp
        import numpy as np
        N_NODES = 6250
        EMBED_DIM = 512
        N_EDGES = 100000
        NEG_SLOPE = 0.01
        key = jax.random.key(seed)
        k1, k2, k3 = jax.random.split(key, 3)
        X = jax.random.normal(k1, (N_NODES, EMBED_DIM), dtype=jnp.float32)
        W = jax.random.normal(k2, (EMBED_DIM, EMBED_DIM), dtype=jnp.float32) / np.sqrt(EMBED_DIM)
        b = jnp.zeros((EMBED_DIM,), dtype=jnp.float32)
        edge_index = jax.random.randint(k3, (2, N_EDGES), 0, N_NODES, dtype=jnp.int32)
        return {'X': X, 'W': W, 'b': b, 'edge_index': edge_index}
    _L3_gnn_all = _L3_gnn_setup()
    _L3_gnn_in = {k: v for k, v in _L3_gnn_all.items() if k in ('W', 'b')}
    del _L3_gnn_all

    def _L3_mix_setup():
        import jax, jax.numpy as jnp
        import numpy as np
        import math
        D_MODEL = 512
        key = jax.random.key(seed)
        k1, k2, k3 = jax.random.split(key, 3)
        X = jax.random.normal(k1, (4, 1024, D_MODEL), dtype=jnp.float32)
        s = 1.0 / math.sqrt(D_MODEL)
        W_v = jax.random.uniform(k2, (D_MODEL, D_MODEL), dtype=jnp.float32, minval=-s, maxval=s)
        W_theta = jax.random.uniform(k3, (D_MODEL, D_MODEL), dtype=jnp.float32, minval=-s, maxval=s)
        return {'X': X, 'W_v': W_v, 'W_theta': W_theta}
    _L3_mix_all = _L3_mix_setup()
    _L3_mix_in = {k: v for k, v in _L3_mix_all.items() if k in ('W_v', 'W_theta')}
    del _L3_mix_all

    def _L3_ffn_setup():
        import jax, jax.numpy as jnp
        import numpy as np
        E = 8
        TOP_K = 2
        H = 512
        DFF = 256
        B, S = (4, 256)
        key = jax.random.key(seed)
        k0, k1, k2, k3 = jax.random.split(key, 4)
        return {'hidden_states': jax.random.normal(k0, (B, S, H), jnp.float32), 'gate_w': jax.random.normal(k1, (E, H), jnp.float32) * 0.01, 'w1': jax.random.normal(k2, (E, H, DFF), jnp.float32) * (1.0 / np.sqrt(H)), 'b1': jnp.zeros((E, DFF), jnp.float32), 'w2': jax.random.normal(k3, (E, DFF, H), jnp.float32) * (1.0 / np.sqrt(DFF)), 'b2': jnp.zeros((E, H), jnp.float32)}
    _L3_ffn_all = _L3_ffn_setup()
    _L3_ffn_in = {k: v for k, v in _L3_ffn_all.items() if k in ('gate_w', 'w1', 'b1', 'w2', 'b2')}
    del _L3_ffn_all
    return {'x': x, 'src': src, 'dst': dst, 'L0_gnn_W': _L0_gnn_in['W'], 'L0_gnn_b': _L0_gnn_in['b'], 'L0_mix_ln1_g': _L0_mix_in['ln1_g'], 'L0_mix_ln1_b': _L0_mix_in['ln1_b'], 'L0_mix_ln2_g': _L0_mix_in['ln2_g'], 'L0_mix_ln2_b': _L0_mix_in['ln2_b'], 'L0_mix_Wq': _L0_mix_in['Wq'], 'L0_mix_bq': _L0_mix_in['bq'], 'L0_mix_Wk': _L0_mix_in['Wk'], 'L0_mix_bk': _L0_mix_in['bk'], 'L0_mix_Wv': _L0_mix_in['Wv'], 'L0_mix_bv': _L0_mix_in['bv'], 'L0_mix_Wo': _L0_mix_in['Wo'], 'L0_mix_bo': _L0_mix_in['bo'], 'L0_mix_proj': _L0_mix_in['proj'], 'L0_mix_W1': _L0_mix_in['W1'], 'L0_mix_b1': _L0_mix_in['b1'], 'L0_mix_W2': _L0_mix_in['W2'], 'L0_mix_b2': _L0_mix_in['b2'], 'L0_ffn_gate_w': _L0_ffn_in['gate_w'], 'L0_ffn_w1': _L0_ffn_in['w1'], 'L0_ffn_b1': _L0_ffn_in['b1'], 'L0_ffn_w2': _L0_ffn_in['w2'], 'L0_ffn_b2': _L0_ffn_in['b2'], 'L0_ffn_sw1': _L0_ffn_in['sw1'], 'L0_ffn_sb1': _L0_ffn_in['sb1'], 'L0_ffn_sw2': _L0_ffn_in['sw2'], 'L0_ffn_sb2': _L0_ffn_in['sb2'], 'L1_gnn_W_l': _L1_gnn_in['W_l'], 'L1_gnn_b_l': _L1_gnn_in['b_l'], 'L1_gnn_W_r': _L1_gnn_in['W_r'], 'L1_gnn_gamma': _L1_gnn_in['gamma'], 'L1_gnn_beta': _L1_gnn_in['beta'], 'L1_mix_norm_w': _L1_mix_in['norm_w'], 'L1_mix_w_qkv': _L1_mix_in['w_qkv'], 'L1_mix_mem_kv': _L1_mix_in['mem_kv'], 'L1_mix_w_out': _L1_mix_in['w_out'], 'L1_mix_b_out': _L1_mix_in['b_out'], 'L1_mix_out_norm_w': _L1_mix_in['out_norm_w'], 'L1_ffn_gw1': _L1_ffn_in['gw1'], 'L1_ffn_gb1': _L1_ffn_in['gb1'], 'L1_ffn_gw2': _L1_ffn_in['gw2'], 'L1_ffn_gb2': _L1_ffn_in['gb2'], 'L1_ffn_we1': _L1_ffn_in['we1'], 'L1_ffn_be1': _L1_ffn_in['be1'], 'L1_ffn_we2': _L1_ffn_in['we2'], 'L1_ffn_be2': _L1_ffn_in['be2'], 'L2_gnn_W1': _L2_gnn_in['W1'], 'L2_gnn_b1': _L2_gnn_in['b1'], 'L2_gnn_W2': _L2_gnn_in['W2'], 'L2_gnn_b2': _L2_gnn_in['b2'], 'L2_mix_Wqkv': _L2_mix_in['Wqkv'], 'L2_mix_Wout': _L2_mix_in['Wout'], 'L2_mix_bout': _L2_mix_in['bout'], 'L2_ffn_gate_w': _L2_ffn_in['gate_w'], 'L2_ffn_w1': _L2_ffn_in['w1'], 'L2_ffn_w2': _L2_ffn_in['w2'], 'L2_ffn_w3': _L2_ffn_in['w3'], 'L2_ffn_n1': _L2_ffn_in['n1'], 'L2_ffn_n2': _L2_ffn_in['n2'], 'L3_gnn_W': _L3_gnn_in['W'], 'L3_gnn_b': _L3_gnn_in['b'], 'L3_mix_W_v': _L3_mix_in['W_v'], 'L3_mix_W_theta': _L3_mix_in['W_theta'], 'L3_ffn_gate_w': _L3_ffn_in['gate_w'], 'L3_ffn_w1': _L3_ffn_in['w1'], 'L3_ffn_b1': _L3_ffn_in['b1'], 'L3_ffn_w2': _L3_ffn_in['w2'], 'L3_ffn_b2': _L3_ffn_in['b2']}

def reference(x, src, dst, L0_gnn_W, L0_gnn_b, L0_mix_ln1_g, L0_mix_ln1_b, L0_mix_ln2_g, L0_mix_ln2_b, L0_mix_Wq, L0_mix_bq, L0_mix_Wk, L0_mix_bk, L0_mix_Wv, L0_mix_bv, L0_mix_Wo, L0_mix_bo, L0_mix_proj, L0_mix_W1, L0_mix_b1, L0_mix_W2, L0_mix_b2, L0_ffn_gate_w, L0_ffn_w1, L0_ffn_b1, L0_ffn_w2, L0_ffn_b2, L0_ffn_sw1, L0_ffn_sb1, L0_ffn_sw2, L0_ffn_sb2, L1_gnn_W_l, L1_gnn_b_l, L1_gnn_W_r, L1_gnn_gamma, L1_gnn_beta, L1_mix_norm_w, L1_mix_w_qkv, L1_mix_mem_kv, L1_mix_w_out, L1_mix_b_out, L1_mix_out_norm_w, L1_ffn_gw1, L1_ffn_gb1, L1_ffn_gw2, L1_ffn_gb2, L1_ffn_we1, L1_ffn_be1, L1_ffn_we2, L1_ffn_be2, L2_gnn_W1, L2_gnn_b1, L2_gnn_W2, L2_gnn_b2, L2_mix_Wqkv, L2_mix_Wout, L2_mix_bout, L2_ffn_gate_w, L2_ffn_w1, L2_ffn_w2, L2_ffn_w3, L2_ffn_n1, L2_ffn_n2, L3_gnn_W, L3_gnn_b, L3_mix_W_v, L3_mix_W_theta, L3_ffn_gate_w, L3_ffn_w1, L3_ffn_b1, L3_ffn_w2, L3_ffn_b2):
    import jax
    import jax.numpy as jnp

    def _L0_gnn_ref(x, edge_index, W, b):
        import jax, jax.numpy as jnp
        import numpy as np
        N_NODES = 6250
        N_EDGES = 50000
        IN_DIM = 512
        OUT_DIM = 512
        n = x.shape[0]
        loops = jnp.arange(n, dtype=edge_index.dtype)
        row = jnp.concatenate([edge_index[0], loops])
        col = jnp.concatenate([edge_index[1], loops])
        deg = jax.ops.segment_sum(jnp.ones(row.shape[0], dtype=x.dtype), row, num_segments=n)
        dis = jax.lax.rsqrt(deg)
        norm = dis[row] * dis[col]
        h = x @ W.T + b
        out = jax.ops.segment_sum(norm[:, None] * h[row], col, num_segments=n)
        return jax.nn.relu(out)

    def _L0_mix_ref(x, ln1_g, ln1_b, ln2_g, ln2_b, Wq, bq, Wk, bk, Wv, bv, Wo, bo, proj, W1, b1, W2, b2):
        import jax, jax.numpy as jnp
        import numpy as np
        DEPTH, DIM, HEADS, DIM_HEAD, NBF, MULT = (2, 512, 8, 64, 256, 4)
        INNER = HEADS * DIM_HEAD

        def layernorm(x, g, b, eps=1e-05):
            mu = jnp.mean(x, axis=-1, keepdims=True)
            var = jnp.mean((x - mu) ** 2, axis=-1, keepdims=True)
            return (x - mu) * jax.lax.rsqrt(var + eps) * g + b

        def softmax_kernel(data, proj, is_query, eps=0.0001):
            d = data.shape[-1]
            normalizer = d ** (-0.25)
            ratio = proj.shape[0] ** (-0.5)
            data_dash = jnp.einsum('bhnd,md->bhnm', data * normalizer, proj)
            diag = jnp.sum(data ** 2, axis=-1, keepdims=True) * 0.5 * normalizer ** 2
            if is_query:
                m = jnp.max(data_dash, axis=-1, keepdims=True)
            else:
                m = jnp.max(data_dash, axis=(-2, -1), keepdims=True)
            m = jax.lax.stop_gradient(m)
            return ratio * (jnp.exp(data_dash - diag - m) + eps)
        B, N, D = x.shape
        for i in range(DEPTH):
            y = layernorm(x, ln1_g[i], ln1_b[i])
            q = (y @ Wq[i] + bq[i]).reshape(B, N, HEADS, DIM_HEAD).transpose(0, 2, 1, 3)
            k = (y @ Wk[i] + bk[i]).reshape(B, N, HEADS, DIM_HEAD).transpose(0, 2, 1, 3)
            v = (y @ Wv[i] + bv[i]).reshape(B, N, HEADS, DIM_HEAD).transpose(0, 2, 1, 3)
            qp = softmax_kernel(q, proj[i], True)
            kp = softmax_kernel(k, proj[i], False)
            k_sum = kp.sum(axis=2)
            d_inv = 1.0 / jnp.einsum('bhnm,bhm->bhn', qp, k_sum)
            ctx = jnp.einsum('bhnm,bhnd->bhmd', kp, v)
            o = jnp.einsum('bhmd,bhnm,bhn->bhnd', ctx, qp, d_inv)
            o = o.transpose(0, 2, 1, 3).reshape(B, N, INNER)
            x = x + o @ Wo[i] + bo[i]
            y = layernorm(x, ln2_g[i], ln2_b[i])
            h = jax.nn.gelu(y @ W1[i] + b1[i], approximate=False)
            x = x + h @ W2[i] + b2[i]
        return x

    def _L0_ffn_ref(hidden_states, gate_w, w1, b1, w2, b2, sw1, sb1, sw2, sb2):
        import jax, jax.numpy as jnp
        import numpy as np
        B, S, H, E, K, DF, SH = (8, 512, 512, 8, 2, 128, 512)
        x = hidden_states
        xf = x.reshape(-1, x.shape[-1])
        T = xf.shape[0]
        scores = jax.nn.softmax(xf @ gate_w.T, axis=-1)
        topk_w, topk_i = jax.lax.top_k(scores, K)
        topk_w = topk_w / (topk_w.sum(-1, keepdims=True) + 1e-20)
        combine = jnp.zeros((T, E), xf.dtype).at[jnp.arange(T)[:, None], topk_i].add(topk_w)
        h1 = jax.nn.relu(jnp.einsum('th,ehf->tef', xf, w1) + b1)
        eo = jnp.einsum('tef,efh->teh', h1, w2) + b2
        y = jnp.einsum('te,teh->th', combine, eo)
        shared = jax.nn.relu(xf @ sw1 + sb1) @ sw2 + sb2
        return (y + shared).reshape(x.shape)

    def _L1_gnn_ref(x, edge_index, W_l, b_l, W_r, gamma, beta):
        import jax, jax.numpy as jnp
        import numpy as np
        N, E, D = (6250, 50000, 512)
        EPS = 1e-05
        n = x.shape[0]
        src, dst = (edge_index[0], edge_index[1])
        agg = jax.ops.segment_sum(x[src], dst, num_segments=n)
        cnt = jax.ops.segment_sum(jnp.ones((src.shape[0],), x.dtype), dst, num_segments=n)
        mean_agg = agg / jnp.maximum(cnt, 1.0)[:, None]
        h = mean_agg @ W_l.T + b_l + x @ W_r.T
        mu = jnp.mean(h, axis=0)
        var = jnp.var(h, axis=0)
        h = (h - mu) * jax.lax.rsqrt(var + EPS) * gamma + beta
        return jax.nn.relu(h) + x

    def _L1_mix_ref(x, norm_w, w_qkv, mem_kv, w_out, b_out, out_norm_w):
        import jax, jax.numpy as jnp
        import numpy as np
        DIM = 512
        H = 8
        C = 64
        HID = H * C
        NMEM = H

        def _rmsnorm_seq(x, w):
            n = jnp.sqrt(jnp.sum(x * x, axis=2, keepdims=True))
            return x / jnp.maximum(n, 1e-12) * w * jnp.asarray(DIM ** 0.5, x.dtype)
        b, n, _ = x.shape
        scale = jnp.asarray(C ** (-0.5), x.dtype)
        xn = _rmsnorm_seq(x, norm_w)
        qkv = xn @ w_qkv
        q, k, v = jnp.split(qkv, 3, axis=2)

        def to_heads(t):
            return t.reshape(b, n, H, C).transpose(0, 2, 3, 1)
        q, k, v = map(to_heads, (q, k, v))
        mk = jnp.broadcast_to(mem_kv[0], (b, H, C, NMEM))
        mv = jnp.broadcast_to(mem_kv[1], (b, H, C, NMEM))
        k = jnp.concatenate([mk, k], axis=-1)
        v = jnp.concatenate([mv, v], axis=-1)
        q = jax.nn.softmax(q, axis=-2) * scale
        k = jax.nn.softmax(k, axis=-1)
        context = jnp.einsum('bhdn,bhen->bhde', k, v)
        out = jnp.einsum('bhde,bhdn->bhen', context, q)
        out = out.transpose(0, 3, 1, 2).reshape(b, n, HID)
        out = out @ w_out + b_out
        return _rmsnorm_seq(out, out_norm_w)

    def _L1_ffn_ref(x, gw1, gb1, gw2, gb2, we1, be1, we2, be2):
        import jax, jax.numpy as jnp
        import numpy as np
        E = 8
        TOP_K = 2
        D = 512
        H = 1024
        B, S = (16, 512)
        b, s, d = x.shape
        xf = x.reshape(-1, d)
        T = xf.shape[0]
        gate_logits = jax.nn.relu(xf @ gw1 + gb1) @ gw2 + gb2
        gate_weights = jax.nn.softmax(gate_logits, axis=-1)
        top_w, top_idx = jax.lax.top_k(gate_weights, TOP_K)
        top_w = jax.nn.softmax(top_w, axis=-1)
        combine = jnp.zeros((T, E), dtype=xf.dtype)
        combine = combine.at[jnp.arange(T)[:, None], top_idx].add(top_w)
        out = jnp.zeros_like(xf)
        for e in range(E):
            h = jax.nn.gelu(xf @ we1[e] + be1[e], approximate=False)
            y = h @ we2[e] + be2[e]
            out = out + combine[:, e:e + 1] * y
        return out.reshape(b, s, d)

    def _L2_gnn_ref(h, edge_index, W1, b1, W2, b2):
        import jax, jax.numpy as jnp
        import numpy as np
        N_NODES = 1250
        N_EDGES = 20000
        D = 512
        send, rec = (edge_index[0], edge_index[1])
        agg = jax.ops.segment_sum(h[send], rec, num_segments=h.shape[0])
        x = h + agg
        x = jax.nn.relu(x @ W1 + b1)
        x = x @ W2 + b2
        return x

    def _L2_mix_ref(x, Wqkv, Wout, bout):
        import jax, jax.numpy as jnp
        import numpy as np
        HEADS = 8
        DIM_HEAD = 64
        B, L, D = x.shape
        H, C = (HEADS, DIM_HEAD)
        qkv = jnp.einsum('bld,od->bol', x, Wqkv)
        qkv = qkv.reshape(B, 3, H, C, L)
        q, k, v = (qkv[:, 0], qkv[:, 1], qkv[:, 2])
        k = jax.nn.softmax(k, axis=-1)
        q = jax.nn.softmax(q, axis=-2)
        context = jnp.einsum('bhdn,bhen->bhde', k, v)
        out = jnp.einsum('bhde,bhdn->bhen', context, q)
        out = out.reshape(B, H * C, L)
        y = jnp.einsum('bcl,dc->bld', out, Wout) + bout
        return y

    def _L2_ffn_ref(x, gate_w, w1, w2, w3, n1, n2):
        import jax, jax.numpy as jnp
        import numpy as np
        E = 8
        K = 2
        D = 512
        H = 256
        EPS = 1e-06

        def _rmsnorm(x, w):
            return x * jax.lax.rsqrt(jnp.mean(x * x, axis=-1, keepdims=True) + EPS) * w
        B, T, Dm = x.shape
        xf = x.reshape(-1, Dm)
        logits = xf @ gate_w
        tk_logits, tk_idx = jax.lax.top_k(logits, K)
        gates = jax.nn.softmax(tk_logits, axis=-1)
        h1 = jax.nn.gelu(jnp.einsum('nd,edh->enh', xf, w1), approximate=False)
        h1 = _rmsnorm(h1, n1[:, None, :])
        h2 = jax.nn.gelu(jnp.einsum('enh,ehk->enk', h1, w2), approximate=False)
        h2 = _rmsnorm(h2, n2[:, None, :])
        expert_out = jnp.einsum('enh,ehd->ned', h2 + h1, w3)
        sel = jnp.take_along_axis(expert_out, tk_idx[:, :, None], axis=1)
        out = jnp.sum(gates[:, :, None] * sel, axis=1)
        return out.reshape(B, T, Dm)

    def _L3_gnn_ref(X, W, b, edge_index):
        import jax, jax.numpy as jnp
        import numpy as np
        N_NODES = 6250
        EMBED_DIM = 512
        N_EDGES = 100000
        NEG_SLOPE = 0.01
        N = X.shape[0]
        loop = jnp.arange(N, dtype=edge_index.dtype)
        src = jnp.concatenate([edge_index[0], loop])
        dst = jnp.concatenate([edge_index[1], loop])
        deg = jax.ops.segment_sum(jnp.ones_like(dst, dtype=X.dtype), dst, num_segments=N)
        dinv = jnp.where(deg > 0, jax.lax.rsqrt(deg), 0.0)
        norm = dinv[src] * dinv[dst]
        H = X @ W
        msgs = H[src] * norm[:, None]
        out = jax.ops.segment_sum(msgs, dst, num_segments=N) + b
        return jnp.where(out >= 0, out, NEG_SLOPE * out)

    def _L3_mix_ref(X, W_v, W_theta):
        import jax, jax.numpy as jnp
        import numpy as np
        import math
        D_MODEL = 512
        n = X.shape[1]
        d = X.shape[2]
        XW_v = X @ W_v.T
        theta_X = X @ W_theta.T
        first_term = jnp.mean(XW_v, axis=1, keepdims=True)
        kv = jnp.einsum('bnd,bne->bde', theta_X, XW_v)
        second_term = X @ kv / (n * math.sqrt(d))
        return first_term + second_term

    def _L3_ffn_ref(hidden_states, gate_w, w1, b1, w2, b2):
        import jax, jax.numpy as jnp
        import numpy as np
        E = 8
        TOP_K = 2
        H = 512
        DFF = 256
        B, S = (4, 256)
        b, s, h = hidden_states.shape
        flat = hidden_states.reshape(-1, h)
        logits = flat @ gate_w.T
        top_vals, top_idx = jax.lax.top_k(logits, TOP_K)
        top_w = jax.nn.softmax(top_vals, axis=-1)
        combine = jnp.sum(jax.nn.one_hot(top_idx, E, dtype=flat.dtype) * top_w[..., None], axis=1)
        out = jnp.zeros_like(flat)
        for e in range(E):
            hdn = jax.nn.gelu(flat @ w1[e] + b1[e])
            out = out + combine[:, e:e + 1] * (hdn @ w2[e] + b2[e])
        return out.reshape(b, s, h)
    edge_index = jnp.stack([src, dst])
    xn = _layernorm(x, axis=-1)
    x = x + _L0_gnn_ref(xn, edge_index, L0_gnn_W, L0_gnn_b) + _L0_mix_ref(xn[None], L0_mix_ln1_g, L0_mix_ln1_b, L0_mix_ln2_g, L0_mix_ln2_b, L0_mix_Wq, L0_mix_bq, L0_mix_Wk, L0_mix_bk, L0_mix_Wv, L0_mix_bv, L0_mix_Wo, L0_mix_bo, L0_mix_proj, L0_mix_W1, L0_mix_b1, L0_mix_W2, L0_mix_b2)[0]
    x = x + _L0_ffn_ref(_layernorm(x, axis=-1)[None], L0_ffn_gate_w, L0_ffn_w1, L0_ffn_b1, L0_ffn_w2, L0_ffn_b2, L0_ffn_sw1, L0_ffn_sb1, L0_ffn_sw2, L0_ffn_sb2)[0]
    xn = _layernorm(x, axis=-1)
    x = x + _L1_gnn_ref(xn, edge_index, L1_gnn_W_l, L1_gnn_b_l, L1_gnn_W_r, L1_gnn_gamma, L1_gnn_beta) + _L1_mix_ref(xn[None], L1_mix_norm_w, L1_mix_w_qkv, L1_mix_mem_kv, L1_mix_w_out, L1_mix_b_out, L1_mix_out_norm_w)[0]
    x = x + _L1_ffn_ref(_layernorm(x, axis=-1)[None], L1_ffn_gw1, L1_ffn_gb1, L1_ffn_gw2, L1_ffn_gb2, L1_ffn_we1, L1_ffn_be1, L1_ffn_we2, L1_ffn_be2)[0]
    xn = _layernorm(x, axis=-1)
    x = x + _L2_gnn_ref(xn, edge_index, L2_gnn_W1, L2_gnn_b1, L2_gnn_W2, L2_gnn_b2) + _L2_mix_ref(xn[None], L2_mix_Wqkv, L2_mix_Wout, L2_mix_bout)[0]
    x = x + _L2_ffn_ref(_layernorm(x, axis=-1)[None], L2_ffn_gate_w, L2_ffn_w1, L2_ffn_w2, L2_ffn_w3, L2_ffn_n1, L2_ffn_n2)[0]
    xn = _layernorm(x, axis=-1)
    x = x + _L3_gnn_ref(xn, L3_gnn_W, L3_gnn_b, edge_index) + _L3_mix_ref(xn[None], L3_mix_W_v, L3_mix_W_theta)[0]
    x = x + _L3_ffn_ref(_layernorm(x, axis=-1)[None], L3_ffn_gate_w, L3_ffn_w1, L3_ffn_b1, L3_ffn_w2, L3_ffn_b2)[0]
    return x

_drawn_inputs = setup_inputs


def setup_inputs(seed=0):
    import zlib

    import numpy as np

    out = dict(_drawn_inputs(seed))
    spreads = {'L0_mix_ln1_g': (1.0, 0.6),
     'L0_mix_ln1_b': (0.0, 0.1),
     'L0_mix_ln2_g': (1.0, 0.2),
     'L0_mix_ln2_b': (0.0, 0.1),
     'L0_mix_bq': (0.0, 0.8),
     'L0_mix_bk': (0.0, 0.8),
     'L0_mix_bv': (0.0, 0.1),
     'L0_mix_bo': (0.0, 0.1),
     'L0_mix_b1': (0.0, 0.1),
     'L0_mix_b2': (0.0, 0.1),
     'L1_gnn_b_l': (0.0, 2.0),
     'L1_gnn_gamma': (1.0, 0.2),
     'L1_gnn_beta': (0.0, 0.1),
     'L1_mix_norm_w': (1.0, 0.2),
     'L1_mix_out_norm_w': (1.0, 0.2),
     'L1_ffn_gb1': (0.0, 0.502),
     'L1_ffn_gb2': (0.0, 0.316),
     'L1_ffn_be1': (0.0, 0.599),
     'L1_ffn_be2': (0.0, 0.1),
     'L2_gnn_b1': (0.0, 0.587),
     'L2_gnn_b2': (0.0, 0.409),
     'L2_mix_bout': (0.0, 0.381),
     'L2_ffn_n1': (1.0, 0.542),
     'L2_ffn_n2': (1.0, 0.6),
     'L3_gnn_b': (0.0, 0.8),
     'L3_ffn_b1': (0.0, 0.8),
     'L3_ffn_b2': (0.0, 0.8)}
    factors = {'L0_gnn_b': 6.027,
     'L0_mix_Wq': 7.75,
     'L0_mix_Wk': 8.0,
     'L0_mix_proj': 8.0,
     'L0_ffn_b1': 23.534,
     'L0_ffn_b2': 7.525,
     'L0_ffn_sb1': 5.267,
     'L0_ffn_sb2': 3.286,
     'L1_mix_mem_kv': 8.0,
     'L3_mix_W_theta': 3.271}
    for name, (base, spread) in spreads.items():
        noise = np.random.default_rng([zlib.crc32(name.encode()), seed]).standard_normal(out[name].shape)
        drawn = base * np.exp(spread * noise) if base else spread * noise
        out[name] = jnp.asarray(drawn.astype(out[name].dtype))
    for name, factor in factors.items():
        out[name] = (out[name] * factor).astype(out[name].dtype)
    return out
```

```python
from contextlib import ExitStack

import concourse.bass as bass
from concourse import mybir
from concourse.alu_op_type import AluOpType as ALU

ACT = mybir.ActivationFunctionType
F32 = mybir.dt.float32
F16 = mybir.dt.float16
I32 = mybir.dt.int32
AX_X = mybir.AxisListType.X

N = 1250
D = 512
T = 10
R = N // T
KC = D // 128
CH = [(0, 4), (4, 4), (8, 2)]
E_EDGES = 20000
EC = E_EDGES // R
EROWS = EC // 2
HEADS, DH, NBF = 8, 64, 256
NE = 8
DA = DH + 1
UNIT_SLOTS = 3
EH_SLOTS = 4
LN_EPS = 1e-5
BIG = 1e30

COLS = {}
for _i in range(2):
    for _n, _w in (("ln1g", 4), ("ln1b", 4), ("ln2g", 4), ("ln2b", 4), ("bq", 4), ("bk", 4), ("b1", 16)):
        COLS[f"L0{_n}{_i}"] = _w
for _n, _w in (("L0eb1", 8), ("L0sb1", 4), ("L1bl", 4), ("L1gamma", 4), ("L1beta", 4), ("L1nw", 4),
               ("L1gb1", 2), ("L1be1", 64), ("L2b1", 4), ("L2n1", 16), ("L2n2", 16), ("L3eb1", 16),
               ("L0gate", 32), ("L1gate", 16), ("L2gate", 32), ("L3gate", 32), ("memk", 32), ("memv", 32)):
    COLS[_n] = _w
COL_AT = {}
_at = 0
for _n, _w in COLS.items():
    COL_AT[_n] = _at
    _at += _w
NCOLS = _at

ROWS = ["L0gb", "bv0", "bo0", "b20", "bv1", "bo1", "b21", "E0", "L0sb2", "L1bout", "L1onw", "gb2", "E1",
        "L2gb2", "L2bout", "L3gb", "E2"]
VEC_ROWS = [n for n in ROWS if n[0] != "E" and n != "gb2"]

N_UNITS = 1 + 24 + 6 + 2 + 4 + 33 + 2 + 4 + 10 + 1 + 2 + 8


def build(nc, x_in, src_in, dst_in, units_in, cols_in, rows_in, eb_in, gb2_in, proj_in, out):
    ctx = ExitStack()
    with ctx:
        def sb(name, shape, dt=F32):
            return ctx.enter_context(nc.sbuf_tensor(name, shape, dt))

        sems = {}

        def sem(name):
            if name not in sems:
                sems[name] = ctx.enter_context(nc.semaphore(name))
            return sems[name]

        X = sb("X", [128, T * D])
        M = sb("M", [128, T * D])
        Y = sb("Y", [128, T * HEADS * DA])
        YT = sb("YT", [128, T * D])
        Q = sb("Q", [128, KC * N])
        K = sb("K", [128, KC * N])
        AT = sb("AT", [128, T * N])
        units = sb("units", [128, UNIT_SLOTS, KC * D])
        row_slot = sb("row_slot", [128, D])
        cols = sb("cols", [128, NCOLS])
        proj = sb("proj", [128, 2, 2 * NBF])
        ident = sb("ident", [128, 128])
        ones = sb("ones", [128, 128])
        tmp = sb("tmp", [128, 2, D])
        sel = sb("sel", [128, KC, HEADS])
        stats = sb("stats", [128, 12, 6])
        mv = sb("mv", [128, T, 2])
        std = sb("std", [128, T])
        rstd = sb("rstd", [128, T])
        diag = sb("diag", [128, T * HEADS])
        kmx = sb("kmx", [128, T * HEADS])
        nb = sb("nb", [128, T * HEADS])
        small = sb("small", [128, 64])
        comb = sb("comb", [128, T * NE])
        indeg3 = sb("indeg3", [128, T, 3])
        indeg = sb("indeg", [128, T])
        outdeg = sb("outdeg", [128, T])
        dis = sb("dis", [128, T])
        rcnt = sb("rcnt", [128, T])
        dinv = sb("dinv", [128, T])
        consts = sb("consts", [128, 4])
        colsT = sb("colsT", [128, 8])
        PS = [ctx.enter_context(nc.psum_tensor(f"ps{i}", [128, 512], F32)) for i in range(8)]
        RING = {"act": [0, 1, 2], "dve": [3, 4, 5], "both": [6, 7]}
        A_BANKS = [3, 4, 5]

        def nat(buf, t, a=0, b=D):
            return buf[0:R, t * D + a:t * D + b]

        def tr(buf, k, t0, nt, p=128):
            return buf[0:p, k * N + t0 * R:k * N + (t0 + nt) * R]

        def vaug(t, h, n=1):
            return Y[0:R, (t * HEADS + h) * DA:(t * HEADS + h + n) * DA]

        def col(name, i=0, n=1, p=128):
            return cols[0:p, COL_AT[name] + i:COL_AT[name] + i + n]

        def at(s, a, b):
            return AT[0:R, s * N + a:s * N + b]

        def small_k(i):
            return K[0:R, i * T * NE:(i + 1) * T * NE].rearrange("p (t e) -> p t e", e=NE)

        combT = K[0:NE, N:2 * N]
        comb3 = comb[0:R, :].rearrange("p (t e) -> p t e", e=NE)
        EPS_LN, EPS_PHI, EPS_RMS = consts[:, 0:1], consts[:, 1:2], consts[:, 2:3]
        kp_slot = [Q[0:R, i * D:(i + 1) * D] for i in range(4)]
        ctxv = Q[:, 4 * D:4 * D + HEADS * 2 * DA].rearrange("p (h m a) -> p h m a", m=2, a=DA)
        qp_slot = [Q[0:R, 3200 + i * D:3200 + (i + 1) * D] for i in range(3)]
        qpT_slot = [tmp[:, i, 0:4 * R].rearrange("p (j r) -> p j r", r=R) for i in range(2)]
        iota_i = YT[0:R, 0:N].bitcast(I32)
        iota16 = YT[0:R, N:N + N // 2].bitcast(F16)
        zero16 = YT[0:R, 2000:2064].bitcast(F16)
        ohs = [Q[0:R, i * 640:i * 640 + N // 2].bitcast(F16) for i in range(EH_SLOTS)]
        ohd = [Q[0:R, 2600 + i * 64:2600 + i * 64 + 64].bitcast(F16) for i in range(EH_SLOTS)]
        edges_i = [K[0:EROWS, i * 250:(i + 1) * 250].bitcast(I32) for i in range(2)]
        edges_f = [K[0:EROWS, 500 + i * 250:500 + (i + 1) * 250] for i in range(2)]
        edgesT = [K[0:R, 1000 + i * EC:1000 + (i + 1) * EC] for i in range(2)]
        a_nat = K[0:R, 1400:1400 + N]
        dg8 = small[0:8, 0:8]
        km8 = small[0:8, 8:9]
        kh = small[0:R, 16:24]
        rec2 = [small[0:R, 24 + 2 * i:26 + 2 * i] for i in range(4)]
        G = Q[:, 0:KC * D]
        P_ = K[:, 0:KC * D]
        KV = Y[:, 0:KC * D]
        GATE_D = small[0:R, 48:48 + T]
        kneg = colsT[:, 0:4]
        ksum = colsT[:, 4:8]
        ksum2 = small[:, 0:4]
        bd = YT[:, 0:D]

        unit_release = []
        row_release = []

        class Tally:

            def __init__(self):
                self.seen, self.sent, self.last = {}, {}, None

            def more(self, name, n=1):
                self.seen[name] = self.seen.get(name, 0) + n
                return self.seen[name]

            def one(self, name):
                self.sent[name] = self.sent.get(name, 0) + 1
                self.last = (name, self.sent[name])
                return 1

            def latest(self):
                return sem(self.last[0]), self.last[1]

            def bank(self, ring):
                return PS[RING[ring][(self.seen[f"filled_{ring}"] - 1) % len(RING[ring])]]

        block = ctx.enter_context(nc.Block())

        @block.tensor
        def _(pe):
            s = Tally()
            given = {r: [] for r in RING}
            promised = {}

            def left(ring):
                log = given[ring]
                if len(log) < len(RING[ring]):
                    return sem("ident"), 1
                before, value = log[len(log) - len(RING[ring])]
                return sem(before), value

            def bank(ring, name):
                log = given[ring]
                promised[name] = promised.get(name, 0) + 1
                log.append((name, promised[name]))
                return PS[RING[ring][(len(log) - 1) % len(RING[ring])]]

            def loaded():
                u = len(unit_release)
                return sem(f"unit_loaded{u % UNIT_SLOTS}"), 16 * (u // UNIT_SLOTS + 1)

            def unit():
                u = len(unit_release)
                unit_release.append(None)
                return u, units[:, u % UNIT_SLOTS, :].rearrange("p (k n) -> p k n", k=KC)

            def free(u, ring):
                unit_release[u] = (f"filled_{ring}", len(given[ring]))

            def transposes_T(src, src_name, name, ring="act"):
                for t0, nt in CH:
                    pe.wait_ge(sem(src_name), s.more(src_name, nt))
                    for k in range(KC):
                        pe.wait_ge(*left(ring))
                        o = bank(ring, name)
                        for j in range(nt):
                            ins = pe.transpose(o[:, j * R:(j + 1) * R], src(t0 + j, k * 128, (k + 1) * 128),
                                               ident[0:R, 0:R])
                        ins.then_inc(sem(f"filled_{ring}"), 1)

            def transposes_N(src, src_name, name, ring):
                pe.wait_ge(sem(src_name), s.more(src_name, 12))
                for t in range(T):
                    pe.wait_ge(*left(ring))
                    o = bank(ring, name)
                    for k in range(KC):
                        ins = pe.transpose(o[0:R, k * 128:(k + 1) * 128], tr(src, k, t, 1), ident[:, :])
                    ins.then_inc(sem(f"filled_{ring}"), 1)

            def gemm_T(terms, name, n_oc=4, ring="act"):
                for oc in range(n_oc):
                    for t0, nt in CH:
                        if oc == 0:
                            for _, _, _, need in terms:
                                if need:
                                    pe.wait_ge(sem(need), s.more(need, 4))
                        pe.wait_ge(*left(ring))
                        o = bank(ring, name)
                        steps = [(w(k, oc), m(k, t0, nt)) for w, m, ks, _ in terms for k in ks]
                        for i, (w, m) in enumerate(steps):
                            ins = pe.matmul(o[:, 0:nt * R], w, m, start=(i == 0), stop=(i == len(steps) - 1))
                        ins.then_inc(sem(f"filled_{ring}"), 1)

            def w_of(u):
                return lambda k, oc: u[:, k, oc * 128:(oc + 1) * 128]

            def gemm_N(srcT, w, name, ks=range(KC), width=D):
                ks = list(ks)
                for t in range(T):
                    pe.wait_ge(*left("dve"))
                    o = bank("dve", name)
                    for i, k in enumerate(ks):
                        ins = pe.matmul(o[0:R, 0:width], tr(srcT, k, t, 1), w(k), start=(i == 0), stop=(i == len(ks) - 1))
                    ins.then_inc(sem("filled_dve"), 1)

            def gather_N(src, src_name, name):
                if src_name:
                    pe.wait_ge(sem(src_name), s.more(src_name, T))
                for dt in range(T):
                    pe.wait_ge(*left("dve"))
                    o = bank("dve", name)
                    for k in range(T):
                        ins = pe.matmul(o[0:R, :], at(k, dt * R, (dt + 1) * R), nat(src, k), start=(k == 0), stop=(k == T - 1))
                    ins.then_inc(sem("filled_dve"), 1)

            pe.wait_ge(sem("ident"), s.more("ident", 1))
            pe.wait_ge(sem("cols_loaded"), s.more("cols_loaded", 16))
            pe.wait_ge(sem("consts_set"), s.more("consts_set", 1))
            pe.wait_ge(sem("edges_f"), s.more("edges_f", 2))
            for e in range(2):
                pe.wait_ge(*left("act"))
                o = bank("act", "edgesT")
                for half in range(2):
                    ins = pe.transpose(o[0:R, half * EROWS:(half + 1) * EROWS], edges_f[e][:, half * R:(half + 1) * R],
                                       ident[0:EROWS, 0:EROWS])
                ins.then_inc(sem("filled_act"), 1)
            pe.wait_ge(sem("iota16"), s.more("iota16", 1))
            psA = [PS[b] for b in A_BANKS]
            SPAN = [(0, 500), (500, 1000), (1000, N)]
            for i in range(EH_SLOTS):
                pe.nop().then_inc(sem("onehot_used"), 1)
            for dt in range(T):
                for b, (a0, a1) in enumerate(SPAN):
                    pe.matmul(psA[b][0:R, 0:a1 - a0], zero16[:, 0:R], iota16[:, a0:a1], start=True, stop=False)
                with pe.Fori(0, EC // EH_SLOTS) as it:
                    for j in range(EH_SLOTS):
                        pe.wait_ge(sem("onehot"), it * EH_SLOTS + (dt * EC + j + 1))
                        for b, (a0, a1) in enumerate(SPAN):
                            ins = pe.matmul(psA[b][0:R, 0:a1 - a0], ohd[j][:, 0:R], ohs[j][:, a0:a1], start=False, stop=False)
                        ins.then_inc(sem("onehot_used"), 1)
                for b, (a0, a1) in enumerate(SPAN):
                    ins = pe.matmul(psA[b][0:R, 0:a1 - a0], zero16[:, 0:R], iota16[:, a0:a1], start=False, stop=True)
                ins.then_inc(sem("A_filled"), 1)
                pe.wait_ge(sem("A_nat"), s.more("A_nat", 1))
                for t0, nt in CH:
                    pe.wait_ge(*left("act"))
                    o = bank("act", "AT")
                    for j in range(nt):
                        ins = pe.transpose(o[0:R, j * R:(j + 1) * R], a_nat[:, (t0 + j) * R:(t0 + j + 1) * R], ident[0:R, 0:R])
                    ins.then_inc(sem("filled_act"), 1)

            transposes_T(lambda t, a, b: nat(M, t, a, b), "xn", "yT")
            pe.wait_ge(sem("AT"), s.more("AT", 3 * T))
            pe.wait_ge(sem("yT"), s.more("yT", 12))
            pe.wait_ge(*loaded())
            u, w = unit()
            gemm_N(YT, lambda k: w[:, k, :], "hs0")
            free(u, "dve")
            gather_N(Y, "hs", "gnn")

            pe.wait_ge(sem("proj_scaled"), s.more("proj_scaled", 1))

            def head_pair(buf, t, hp, o):
                return pe.matmul(o[0:R, :], tr(buf, hp, t, 1), proj[:, dep, :], start=True, stop=True)

            def row_norms(sq):
                pe.wait_ge(sem("sqT"), s.more("sqT", 12))
                pe.wait_ge(*left("dve"))
                o = bank("dve", "diag")
                for t in range(T):
                    for c in range(KC):
                        ins = pe.matmul(o[0:R, t * 8:t * 8 + 8], tr(sq, c, t, 1), sel[:, c, :], start=(c == 0), stop=(c == KC - 1))
                ins.then_inc(sem("filled_dve"), 1)

            for dep in range(2):
                transposes_T(lambda t, a, b: nat(Y, t, a, b), "y", "yT")
                pe.wait_ge(*loaded())
                u, w = unit()
                gemm_T([(w_of(w), lambda k, t0, nt: tr(YT, k, t0, nt), range(KC), "yT")], "kT")
                free(u, "act")
                pe.wait_ge(*loaded())
                u, w = unit()
                gemm_N(YT, lambda k: w[:, k, :], "v")
                free(u, "dve")
                row_norms(Q)
                pe.wait_ge(sem("kT"), s.more("kT", 12))
                for t in range(T):
                    for hp in range(4):
                        pe.wait_ge(*left("dve"))
                        head_pair(K, t, hp, bank("dve", "kmax")).then_inc(sem("filled_dve"), 1)
                pe.wait_ge(sem("kh"), s.more("kh", 1))
                pe.wait_ge(*left("dve"))
                o = bank("dve", "km8")
                pe.transpose(o[0:8, 0:R], kh, ident[0:R, 0:R]).then_inc(sem("filled_dve"), 1)
                pe.wait_ge(sem("dg8"), s.more("dg8", 1))
                pe.wait_ge(*left("dve"))
                o = bank("dve", "knb")
                pe.matmul(o[0:R, 0:8], ones[0:8, 0:R], dg8, start=True, stop=True).then_inc(sem("filled_dve"), 1)
                pe.wait_ge(sem("v"), s.more("v", T))
                for hp in range(4):
                    for t in range(T + 2):
                        if t < T:
                            pe.wait_ge(*left("act"))
                            head_pair(K, t, hp, bank("act", "kp")).then_inc(sem("filled_act"), 1)
                        if t >= 2:
                            tt = t - 2
                            if tt == 0:
                                pe.wait_ge(*left("dve"))
                                oc = bank("dve", "ctx")
                            pe.wait_ge(sem("kpe"), s.more("kpe", 1))
                            sl = kp_slot[(hp * T + tt) % 4]
                            for h2 in range(2):
                                for mc in range(2):
                                    a = h2 * 2 + mc
                                    ins = pe.matmul(oc[:, a * DA:(a + 1) * DA], sl[:, a * 128:(a + 1) * 128],
                                                    vaug(tt, 2 * hp + h2), start=(tt == 0 and a == 0),
                                                    stop=(tt == T - 1 and a == 3), skip_group_check=True)
                    ins.then_inc(sem("filled_dve"), 1)
                pe.wait_ge(*loaded())
                u, w = unit()
                gemm_T([(w_of(w), lambda k, t0, nt: tr(YT, k, t0, nt), range(KC), None)], "qT")
                free(u, "act")
                row_norms(YT)
                pe.wait_ge(sem("qT"), s.more("qT", 12))
                pe.wait_ge(sem("ctx"), s.more("ctx", 4))
                for i in range(T * 4 + 3):
                    if i < T * 4:
                        pe.wait_ge(*left("both"))
                        head_pair(K, i // 4, i % 4, bank("both", "qp")).then_inc(sem("filled_both"), 1)
                    if 2 <= i < T * 4 + 2:
                        pe.wait_ge(sem("qp"), s.more("qp", 1))
                        pe.wait_ge(*left("act"))
                        o = bank("act", "qpT")
                        for a in range(4):
                            ins = pe.transpose(o[:, a * R:(a + 1) * R], qp_slot[(i - 2) % 3][:, a * 128:(a + 1) * 128], ident[0:R, 0:R])
                        ins.then_inc(sem("filled_act"), 1)
                    if i >= 3:
                        t, hp = (i - 3) // 4, (i - 3) % 4
                        pe.wait_ge(sem("qpT"), s.more("qpT", 1))
                        pe.wait_ge(*left("dve"))
                        o = bank("dve", "o")
                        for h2 in range(2):
                            for mc in range(2):
                                ins = pe.matmul(o[0:R, h2 * DA:(h2 + 1) * DA], qpT_slot[(i - 3) % 2][:, h2 * 2 + mc, :],
                                                ctxv[:, 2 * hp + h2, mc, :], start=(mc == 0), stop=(mc == 1))
                        ins.then_inc(sem("filled_dve"), 1)
                for t0, nt in CH:
                    pe.wait_ge(sem("o"), s.more("o", 4 * nt))
                    for k in range(KC):
                        pe.wait_ge(*left("act"))
                        o = bank("act", "oT")
                        for j in range(nt):
                            ins = pe.transpose(o[:, j * R:(j + 1) * R], nat(YT, t0 + j, k * 128, (k + 1) * 128), ident[0:R, 0:R])
                        ins.then_inc(sem("filled_act"), 1)
                pe.wait_ge(sem("oT"), s.more("oT", 12))
                pe.wait_ge(*loaded())
                u, w = unit()
                gemm_N(K, lambda k: w[:, k, :], "m_attn")
                free(u, "dve")
                transposes_T(lambda t, a, b: nat(Y, t, a, b), "y", "yT")
                for b in range(4):
                    pe.wait_ge(*loaded())
                    u, w = unit()
                    gemm_T([(w_of(w), lambda k, t0, nt: tr(YT, k, t0, nt), range(KC), "yT" if b == 0 else None)], "hT")
                    free(u, "act")
                    pe.wait_ge(*loaded())
                    u, w = unit()
                    pe.wait_ge(sem("hT"), s.more("hT", 12))
                    gemm_N(Q, lambda k: w[:, k, :], "m_ffn")
                    free(u, "dve")

            def gates(srcT, src_name, src_n, gate, ks):
                if src_name:
                    pe.wait_ge(sem(src_name), s.more(src_name, src_n))
                pe.wait_ge(*left("dve"))
                o = bank("dve", "logits")
                for t in range(T):
                    for k in range(ks):
                        ins = pe.matmul(o[0:R, t * 8:t * 8 + 8], tr(srcT, k, t, 1), col(gate, k * 8, 8), start=(k == 0), stop=(k == ks - 1))
                ins.then_inc(sem("filled_dve"), 1)

            def expert_biases(row):
                pe.wait_ge(sem("comb"), s.more("comb", 1))
                for t0, nt in CH:
                    pe.wait_ge(*left("act"))
                    o = bank("act", "combT")
                    for j in range(nt):
                        ins = pe.transpose(o[0:8, j * R:(j + 1) * R], comb3[:, t0 + j, :], ident[0:R, 0:R])
                    ins.then_inc(sem("filled_act"), 1)
                pe.wait_ge(sem("combT"), s.more("combT", 3))
                pe.wait_ge(sem("row_loaded"), 16 * (ROWS.index(row) + 1))
                for t in range(T):
                    pe.wait_ge(*left("dve"))
                    o = bank("dve", "moe_bias")
                    pe.matmul(o[0:R, :], combT[:, t * R:(t + 1) * R], row_slot[0:8, :], start=True, stop=True).then_inc(sem("filled_dve"), 1)

            def experts(n_units, per_unit, name="moe"):
                for b in range(n_units):
                    pe.wait_ge(*loaded())
                    u, w = unit()
                    gemm_T([(w_of(w), lambda k, t0, nt: tr(YT, k, t0, nt), range(KC), None)], "hT")
                    free(u, "act")
                    pe.wait_ge(*loaded())
                    u, w = unit()
                    pe.wait_ge(sem("hT"), s.more("hT", 12))
                    n = KC // per_unit
                    for e in range(per_unit):
                        gemm_N(Q, lambda k: w[:, k, :], name, range(e * n, e * n + n))
                    free(u, "dve")

            transposes_T(lambda t, a, b: nat(Y, t, a, b), "y", "yT")
            gates(YT, "yT", 12, "L0gate", KC)
            expert_biases("E0")
            experts(2, 4)
            experts(1, 1, "shared")

            transposes_T(lambda t, a, b: nat(M, t, a, b), "xn", "yT")
            gather_N(M, None, "agg")
            transposes_T(lambda t, a, b: nat(Y, t, a, b), "agg", "aggT")
            pe.wait_ge(*loaded())
            u, wl = unit()
            pe.wait_ge(*loaded())
            u2, wr = unit()
            gemm_T([(w_of(wl), lambda k, t0, nt: tr(K, k, t0, nt), range(KC), "aggT"),
                    (w_of(wr), lambda k, t0, nt: tr(YT, k, t0, nt), range(KC), "yT")], "bnT")
            free(u, "act")
            free(u2, "act")
            transposes_N(Q, "bn_out", "gnn", "dve")

            def linear_attention(layer):
                mem = layer == 1
                pe.wait_ge(*loaded())
                u, w = unit()
                gemm_N(YT, lambda k: w[:, k, :], "qsub")
                free(u, "dve")
                transposes_T(lambda t, a, b: nat(Y, t, a, b), "qn", "qT2")
                pe.wait_ge(*loaded())
                u, w = unit()
                gemm_T([(w_of(w), lambda k, t0, nt: tr(YT, k, t0, nt), range(KC), None)], "kT2")
                free(u, "act")
                pe.wait_ge(*loaded())
                u, w = unit()
                gemm_N(YT, lambda k: w[:, k, :], "v2")
                free(u, "dve")
                if mem:
                    pe.wait_ge(sem("kexp"), s.more("kexp", 1))
                    pe.wait_ge(*left("act"))
                    o = bank("act", "memkn")
                    for k in range(KC):
                        ins = pe.transpose(o[0:8, k * 128:(k + 1) * 128], col("memk", k * 8, 8), ident[:, :])
                    ins.then_inc(sem("filled_act"), 1)
                    pe.wait_ge(*left("act"))
                    o = bank("act", "memvn")
                    for k in range(KC):
                        ins = pe.transpose(o[0:8, k * 128:(k + 1) * 128], col("memv", k * 8, 8), ident[:, :])
                    ins.then_inc(sem("filled_act"), 1)
                else:
                    pe.wait_ge(sem("kexp"), s.more("kexp", 1))
                for t in range(T):
                    pe.wait_ge(*left("act"))
                    o = bank("act", "kn")
                    for k in range(KC):
                        ins = pe.transpose(o[0:R, k * 128:(k + 1) * 128], tr(K, k, t, 1), ident[:, :])
                    ins.then_inc(sem("filled_act"), 1)
                pe.wait_ge(sem("v2"), s.more("v2", T))
                pe.wait_ge(sem("kn"), s.more("kn", T))
                if mem:
                    pe.wait_ge(sem("memvn"), s.more("memvn", 1))
                for hp in range(4):
                    a, b = hp * 128, (hp + 1) * 128
                    pe.wait_ge(*left("dve"))
                    o = bank("dve", "ctx2")
                    for t in range(T):
                        ins = pe.matmul(o[:, 0:128], nat(Y, t, a, b), nat(M, t, a, b), start=(t == 0), stop=(t == T - 1 and not mem))
                    if mem:
                        ins = pe.matmul(o[:, 0:128], tmp[0:8, 0, a:b], tmp[0:8, 1, a:b], start=False, stop=True)
                    ins.then_inc(sem("filled_dve"), 1)
                pe.wait_ge(sem("ctx2"), s.more("ctx2", 4))
                pe.wait_ge(sem("qT2"), s.more("qT2", 12))
                for hp in range(4):
                    for t0, nt in CH:
                        pe.wait_ge(*left("act"))
                        o = bank("act", "outT")
                        pe.matmul(o[:, 0:nt * R], bd[:, hp * 128:(hp + 1) * 128], tr(Q, hp, t0, nt), start=True, stop=True).then_inc(sem("filled_act"), 1)
                pe.wait_ge(sem("outT"), s.more("outT", 12))
                pe.wait_ge(*loaded())
                u, w = unit()
                gemm_N(K, lambda k: w[:, k, :], "att_out")
                free(u, "dve")

            transposes_T(lambda t, a, b: nat(Y, t, a, b), "y", "yT")
            pe.wait_ge(sem("yT"), s.more("yT", 12))
            linear_attention(1)

            transposes_T(lambda t, a, b: nat(Y, t, a, b), "y", "yT")
            pe.wait_ge(*loaded())
            u, w = unit()
            gemm_T([(w_of(w), lambda k, t0, nt: tr(YT, k, t0, nt), range(KC), "yT")], "gateT", n_oc=2)
            free(u, "act")
            gates(Q, "gateT", 6, "L1gate", 2)
            expert_biases("E1")
            experts(2 * NE, 1)

            transposes_T(lambda t, a, b: nat(M, t, a, b), "xn", "yT")
            pe.wait_ge(sem("yT"), s.more("yT", 12))
            for k in range(KC):
                for t0, nt in CH:
                    pe.wait_ge(*left("dve"))
                    o = bank("dve", "gT")
                    for q in range(T):
                        ins = pe.matmul(o[:, 0:nt * R], nat(M, q, k * 128, (k + 1) * 128), at(q, t0 * R, (t0 + nt) * R), start=(q == 0), stop=(q == T - 1))
                    ins.then_inc(sem("filled_dve"), 1)
            pe.wait_ge(sem("gT"), s.more("gT", 12))
            pe.wait_ge(*loaded())
            u, w = unit()
            gemm_T([(w_of(w), lambda k, t0, nt: tr(K, k, t0, nt), range(KC), None)], "hT")
            free(u, "act")
            pe.wait_ge(*loaded())
            u, w = unit()
            pe.wait_ge(sem("hT"), s.more("hT", 12))
            gemm_N(Q, lambda k: w[:, k, :], "gnn")
            free(u, "dve")
            linear_attention(2)

            transposes_T(lambda t, a, b: nat(Y, t, a, b), "y", "yT")
            gates(YT, "yT", 12, "L2gate", KC)
            pe.wait_ge(sem("comb"), s.more("comb", 1))
            for pair in range(NE // 2):
                pe.wait_ge(*loaded())
                u, w = unit()
                gemm_T([(w_of(w), lambda k, t0, nt: tr(YT, k, t0, nt), range(KC), None)], "g1T")
                free(u, "act")

                def mean_squares():
                    pe.wait_ge(sem("sqT"), s.more("sqT", 4))
                    for e in range(2):
                        for t0, nt in CH:
                            pe.wait_ge(*left("act"))
                            o = bank("act", "rms")
                            for k in range(2):
                                ins = pe.matmul(o[:, 0:nt * R], ones[:, :], tr(M, 2 * e + k, t0, nt), start=(k == 0), stop=(k == 1))
                            ins.then_inc(sem("filled_act"), 1)
                mean_squares()
                if pair % 2 == 0:
                    pe.wait_ge(*loaded())
                    u2, w2 = unit()
                    w2 = units[:, u2 % UNIT_SLOTS, :].rearrange("p (k n) -> p k n", k=8)
                pe.wait_ge(sem("h1"), s.more("h1", 4))
                for e in range(2):
                    for oc in range(2):
                        for t0, nt in CH:
                            pe.wait_ge(*left("act"))
                            o = bank("act", "g1T")
                            for k in range(2):
                                ins = pe.matmul(o[:, 0:nt * R], w2[:, ((pair % 2) * 2 + e) * 2 + k, oc * 128:(oc + 1) * 128],
                                                tr(K, 2 * e + k, t0, nt), start=(k == 0), stop=(k == 1))
                            ins.then_inc(sem("filled_act"), 1)
                if pair % 2 == 1:
                    free(u2, "act")
                mean_squares()
                pe.wait_ge(*loaded())
                u, w = unit()
                pe.wait_ge(sem("h12"), s.more("h12", 4))
                for e in range(2):
                    gemm_N(K, lambda k: w[:, k, :], "moe", range(2 * e, 2 * e + 2))
                free(u, "dve")

            transposes_T(lambda t, a, b: nat(M, t, a, b), "xn", "yT")
            pe.wait_ge(sem("yT"), s.more("yT", 12))
            pe.wait_ge(*loaded())
            u, w = unit()
            gemm_N(YT, lambda k: w[:, k, :], "hs3")
            free(u, "dve")
            gather_N(Y, "hs3", "gnn")
            for k in range(KC):
                pe.wait_ge(*left("act"))
                o = bank("act", "G")
                for t in range(T):
                    ins = pe.matmul(o[:, :], nat(M, t, k * 128, (k + 1) * 128), nat(M, t), start=(t == 0), stop=(t == T - 1))
                ins.then_inc(sem("filled_act"), 1)
            pe.wait_ge(*left("dve"))
            o = bank("dve", "colsum")
            for k in range(KC):
                for t in range(T):
                    ins = pe.matmul(o[:, k:k + 1], nat(M, t, k * 128, (k + 1) * 128), ones[0:R, 0:1], start=(t == 0), stop=(t == T - 1))
            ins.then_inc(sem("filled_dve"), 1)
            pe.wait_ge(sem("G"), s.more("G", KC))
            pe.wait_ge(*loaded())
            u, w = unit()
            for k in range(KC):
                pe.wait_ge(*left("act"))
                o = bank("act", "P")
                for j in range(KC):
                    ins = pe.matmul(o[:, :], G[:, j * D + k * 128:j * D + (k + 1) * 128], w[:, j, :], start=(j == 0), stop=(j == KC - 1))
                ins.then_inc(sem("filled_act"), 1)
            pe.wait_ge(sem("mean_bc"), s.more("mean_bc", 1))
            pe.wait_ge(*left("dve"))
            o = bank("dve", "first")
            for k in range(KC):
                ins = pe.matmul(o[0:R, :], tmp[:, 0, k * R:(k + 1) * R], w[:, k, :], start=(k == 0), stop=(k == KC - 1))
            ins.then_inc(sem("filled_dve"), 1)
            free(u, "dve")
            pe.wait_ge(sem("P"), s.more("P", KC))
            pe.wait_ge(*loaded())
            u, w = unit()
            for k in range(KC):
                pe.wait_ge(*left("act"))
                o = bank("act", "kv")
                for j in range(KC):
                    ins = pe.matmul(o[:, :], w[:, j, k * 128:(k + 1) * 128], P_[:, j * D:(j + 1) * D], start=(j == 0), stop=(j == KC - 1))
                ins.then_inc(sem("filled_act"), 1)
            free(u, "act")
            pe.wait_ge(sem("kv"), s.more("kv", KC))
            gemm_N(YT, lambda k: KV[:, k * D:(k + 1) * D], "x_mix")
            transposes_T(lambda t, a, b: nat(Y, t, a, b), "y", "yT")
            gates(YT, "yT", 12, "L3gate", KC)
            expert_biases("E2")
            experts(4, 2)
            assert len(unit_release) == N_UNITS

        @block.scalar
        def _(act):
            s = Tally()

            def evac(ring, name, dst, width, func=ACT.Identity, bias=0.0, scale=1.0, p=128):
                act.wait_ge(sem(f"filled_{ring}"), s.more(f"filled_{ring}"))
                o = s.bank(ring)
                act.activation(dst, o[0:p, 0:width], func, bias=bias, scale=scale).then_inc(sem(name), s.one(name))

            def evac_T(dst, name, func=ACT.Identity, bias=None, scale=None, order="c"):
                steps = [(k, c) for c in CH for k in range(KC)] if order == "c" else [(k, c) for k in range(KC) for c in CH]
                for k, (t0, nt) in steps:
                    evac("act", name, tr(dst, k, t0, nt), nt * R, func, bias(k) if bias else 0.0, scale(k) if scale else 1.0)

            def roots(n, src, eps, scale=1.0, dst=None, p=128, name="std"):
                act.activation(dst if dst is not None else std[0:p, 0:n], src, ACT.Sqrt, bias=eps, scale=scale).then_inc(sem(name), s.one(name))

            def ln_root():
                act.wait_ge(sem("mv"), s.more("mv", 1))
                roots(T, mv[0:R, :, 1], EPS_LN[0:R, :], p=R)

            act.wait_ge(sem("consts_set"), s.more("consts_set", 1))
            act.wait_ge(sem("cols_loaded"), s.more("cols_loaded", 16))
            ln_root()
            for e in range(2):
                act.wait_ge(sem("filled_act"), s.more("filled_act"))
                o = s.bank("act")
                act.activation(edgesT[e].rearrange("p (r h) -> p h r", h=2), o[0:R, 0:EC].rearrange("p (h r) -> p h r", h=2),
                                      ACT.Copy).then_inc(sem("edgesT"), s.one("edgesT"))
            for dt in range(T):
                act.wait_ge(sem("A_filled"), s.more("A_filled", 1))
                for b, (a0, a1) in enumerate([(0, 500), (500, 1000), (1000, N)]):
                    ins = act.activation(a_nat[:, a0:a1], PS[A_BANKS[b]][0:R, 0:a1 - a0], ACT.Copy, accum_out=indeg3[0:R, dt, b:b + 1])
                ins.then_inc(sem("A_nat"), s.one("A_nat"))
                for t0, nt in CH:
                    act.wait_ge(sem("filled_act"), s.more("filled_act"))
                    o = s.bank("act")
                    dstv = AT[0:R, :].rearrange("p (s d) -> p s d", s=T)[:, t0:t0 + nt, dt * R:(dt + 1) * R]
                    act.activation(dstv, o[0:R, 0:nt * R].rearrange("p (s d) -> p s d", s=nt), ACT.Copy).then_inc(sem("AT"), s.one("AT"))
            act.wait_ge(*s.latest())
            evac_T(YT, "yT")
            act.wait_ge(sem("degrees"), s.more("degrees", 1))
            act.activation(dis[0:R, :], outdeg[0:R, :], ACT.Sqrt).then_inc(sem("deg_roots"), s.one("deg_roots"))
            act.activation(dinv[0:R, :], indeg[0:R, :], ACT.Sqrt, bias=ones[0:R, 0:1]).then_inc(sem("deg_roots"), s.one("deg_roots"))

            def squares(src, dst):
                for k in range(KC):
                    for t0, nt in CH:
                        act.activation(tr(dst, k, t0, nt), tr(src, k, t0, nt), ACT.Square).then_inc(sem("sqT"), s.one("sqT"))

            for dep in range(2):
                ln_root()
                evac_T(YT, "yT", bias=lambda k: col(f"L0ln1b{dep}", k), scale=lambda k: col(f"L0ln1g{dep}", k))
                evac_T(K, "kT", bias=lambda k: col(f"L0bk{dep}", k), order="k")
                act.wait_ge(*s.latest())
                squares(K, Q)
                act.wait_ge(sem("knb"), s.more("knb", 1))
                for hp in range(4):
                    for t in range(T):
                        act.wait_ge(sem("filled_act"), s.more("filled_act"))
                        o = s.bank("act")
                        for h2 in range(2):
                            h = t * 8 + 2 * hp + h2
                            ins = act.activation(kp_slot[(hp * T + t) % 4][:, h2 * NBF:(h2 + 1) * NBF],
                                                 o[0:R, h2 * NBF:(h2 + 1) * NBF], ACT.Exp, bias=nb[0:R, h:h + 1])
                        ins.then_inc(sem("kp"), s.one("kp"))
                evac_T(K, "qT", bias=lambda k: col(f"L0bq{dep}", k), order="k")
                act.wait_ge(*s.latest())
                squares(K, YT)
                for i in range(T * 4 + 2):
                    if i < T * 4:
                        t, hp = i // 4, i % 4
                        act.wait_ge(sem("filled_both"), s.more("filled_both"))
                        o = s.bank("both")
                        act.wait_ge(sem("qmax"), s.more("qmax", 1))
                        for h2 in range(2):
                            h = t * 8 + 2 * hp + h2
                            ins = act.activation(qp_slot[i % 3][:, h2 * NBF:(h2 + 1) * NBF],
                                                 o[0:R, h2 * NBF:(h2 + 1) * NBF], ACT.Exp, bias=nb[0:R, h:h + 1])
                        ins.then_inc(sem("qp"), s.one("qp"))
                    if i >= 2:
                        evac("act", "qpT", tmp[:, (i - 2) % 2, 0:4 * R], 4 * R, bias=EPS_PHI)
                evac_T(K, "oT")
                ln_root()
                evac_T(YT, "yT", bias=lambda k: col(f"L0ln2b{dep}", k), scale=lambda k: col(f"L0ln2g{dep}", k))
                for b in range(4):
                    evac_T(Q, "hT", ACT.Gelu, bias=lambda k: col(f"L0b1{dep}", 4 * b + k), order="k")

            def gate_exps(n):
                for i in range(n):
                    act.wait_ge(sem(f"gate_in{i}"), s.more(f"gate_in{i}", 1))
                    v = small_k(0) if i == 0 and n == 2 else GATE_D
                    act.activation(v, v, ACT.Exp).then_inc(sem(f"gate_exp{i}"), s.one(f"gate_exp{i}"))

            def combT_evac():
                for t0, nt in CH:
                    evac("act", "combT", combT[:, t0 * R:(t0 + nt) * R], nt * R, p=8)

            ln_root()
            evac_T(YT, "yT")
            act.wait_ge(sem("gate_in0"), s.more("gate_in0", 1))
            act.activation(small_k(0), small_k(0), ACT.Exp).then_inc(sem("gate_exp0"), s.one("gate_exp0"))
            combT_evac()
            for b in range(2):
                evac_T(Q, "hT", ACT.Relu, bias=lambda k: col("L0eb1", 4 * b + k), order="k")
            evac_T(Q, "hT", ACT.Relu, bias=lambda k: col("L0sb1", k), order="k")
            ln_root()
            evac_T(YT, "yT")
            evac_T(K, "aggT")
            evac_T(Q, "bnT", bias=lambda k: col("L1bl", k), order="k")
            act.wait_ge(sem("bn_mv"), s.more("bn_mv", 1))
            roots(KC, mv[:, 0:KC, 1], EPS_LN)
            act.wait_ge(sem("bn_affine"), s.more("bn_affine", 1))
            for k in range(KC):
                act.activation(Q[:, k * N:(k + 1) * N], Q[:, k * N:(k + 1) * N], ACT.Relu,
                                      bias=colsT[:, 4 + k:5 + k], scale=colsT[:, k:k + 1]).then_inc(sem("bn_relu"), s.one("bn_relu"))

            def linear_attention(layer):
                mem = layer == 1
                for t in range(T):
                    act.wait_ge(sem("qsub"), s.more("qsub", 1))
                    act.activation(tmp[0:R, t % 2, :], tmp[0:R, t % 2, :], ACT.Exp).then_inc(sem("qexp"), s.one("qexp"))
                evac_T(Q, "qT2")
                evac_T(K, "kT2", order="k")
                for k in range(KC):
                    act.wait_ge(sem("k_max"), s.more("k_max", 1))
                    ins = act.activation(K[:, k * N:(k + 1) * N], K[:, k * N:(k + 1) * N], ACT.Exp,
                                         bias=kneg[:, k:k + 1], accum_out=ksum[:, k:k + 1])
                    if mem:
                        ins = act.activation(col("memk", k * 8, 8), col("memk", k * 8, 8), ACT.Exp,
                                             bias=kneg[:, k:k + 1], accum_out=ksum2[:, k:k + 1])
                ins.then_inc(sem("kexp"), s.one("kexp"))
                if mem:
                    act.wait_ge(sem("qn_last"), s.more("qn_last", 1))
                    evac("act", "memkn", tmp[0:8, 0, :], D, p=8)
                    evac("act", "memvn", tmp[0:8, 1, :], D, p=8)
                for t in range(T):
                    evac("act", "kn", nat(Y, t), D, p=R)
                evac_T(K, "outT", order="k")
                if mem:
                    for t in range(T):
                        act.wait_ge(sem("att_out"), s.more("att_out", 1))
                        ins = act.activation(nat(M, t), nat(Y, t), ACT.Square, accum_out=small[0:R, 32 + t:33 + t])
                    ins.then_inc(sem("sumsq"), s.one("sumsq"))
                    act.wait_ge(*s.latest())
                    roots(T, small[0:R, 32:32 + T], 0.0, p=R)

            act.wait_ge(sem("xn_all"), s.more("xn_all", 1))
            for t in range(T):
                ins = act.activation(nat(Y, t), nat(M, t), ACT.Square, accum_out=small[0:R, 32 + t:33 + t])
            ins.then_inc(sem("act_sq"), s.one("act_sq"))
            act.wait_ge(*s.latest())
            roots(T, small[0:R, 32:32 + T], 0.0, p=R)
            act.wait_ge(sem("nw_scaled"), s.more("nw_scaled", 1))
            evac_T(YT, "yT", scale=lambda k: col("L1nw", k))
            linear_attention(1)
            ln_root()
            evac_T(YT, "yT")
            for k in range(2):
                for t0, nt in CH:
                    evac("act", "gateT", tr(Q, k, t0, nt), nt * R, ACT.Relu, col("L1gb1", k))
            act.wait_ge(sem("gate_in0"), s.more("gate_in0", 1))
            act.activation(small_k(0), small_k(0), ACT.Exp).then_inc(sem("gate_exp0"), s.one("gate_exp0"))
            act.wait_ge(sem("gate_in1"), s.more("gate_in1", 1))
            act.activation(GATE_D, GATE_D, ACT.Exp).then_inc(sem("gate_exp1"), s.one("gate_exp1"))
            combT_evac()
            for b in range(2 * NE):
                evac_T(Q, "hT", ACT.Gelu, bias=lambda k: col("L1be1", 4 * b + k), order="k")
            ln_root()
            evac_T(YT, "yT")
            evac_T(Q, "hT", ACT.Relu, bias=lambda k: col("L2b1", k), order="k")
            linear_attention(2)
            ln_root()
            evac_T(YT, "yT")
            act.wait_ge(sem("gate_in1"), s.more("gate_in1", 1))
            act.activation(GATE_D, GATE_D, ACT.Exp).then_inc(sem("gate_exp1"), s.one("gate_exp1"))
            for pair in range(NE // 2):
                for half in range(2):
                    evac_T(Q, "g1T", ACT.Gelu, order="k")
                    for e in range(2):
                        for t0, nt in CH:
                            evac("act", "rms", tr(Y, e, t0, nt), nt * R, ACT.Sqrt, EPS_RMS, 1.0 / NBF)
            ln_root()
            evac_T(YT, "yT")
            for k in range(KC):
                evac("act", "G", G[:, k * D:(k + 1) * D], D)
            for k in range(KC):
                evac("act", "P", P_[:, k * D:(k + 1) * D], D)
            act.wait_ge(sem("gnn_read"), s.more("gnn_read", 1))
            for k in range(KC):
                evac("act", "kv", KV[:, k * D:(k + 1) * D], D, scale=1.0 / (N * float(D) ** 0.5))
            ln_root()
            evac_T(YT, "yT")
            act.wait_ge(sem("gate_in1"), s.more("gate_in1", 1))
            act.activation(GATE_D, GATE_D, ACT.Exp).then_inc(sem("gate_exp1"), s.one("gate_exp1"))
            combT_evac()
            for b in range(4):
                evac_T(Q, "hT", ACT.Gelu_apprx_tanh, bias=lambda k: col("L3eb1", 4 * b + k), order="k")

        @block.vector
        def _(dve):
            s = Tally()
            tt, ts, stt = dve.tensor_tensor, dve.tensor_scalar, dve.scalar_tensor_tensor

            def row(name):
                j = ROWS.index(name)
                dve.wait_ge(sem("row_loaded"), 16 * (j + 1))
                return row_slot[0:R, :]

            def row_free(name):
                j = ROWS.index(name)
                assert j == len(row_release)
                row_release.append(s.last)

            def layer_norm(src, dst, name, sig=None):
                for t in range(T):
                    ins = dve.bn_stats(stats[0:R, t, :], nat(src, t))
                ins.then_inc(sem("dve_step"), s.one("dve_step"))
                dve.wait_ge(*s.latest())
                for t in range(T):
                    ins = dve.bn_aggr(mv[0:R, t, :], stats[0:R, t, :])
                ins.then_inc(sem("mv"), s.one("mv"))
                dve.wait_ge(sem("std"), s.more("std", 1))
                dve.reciprocal(rstd[0:R, :], std[0:R, 0:T]).then_inc(sem("dve_step"), s.one("dve_step"))
                dve.wait_ge(*s.latest())
                for t in range(T):
                    ts(nat(dst, t), nat(src, t), mv[0:R, t, 0:1], rstd[0:R, t:t + 1], ALU.subtract, ALU.mult).then_inc(sem(name), s.one(name))
                dve.wait_ge(*s.latest())

            def add_to(dst, name, bias=None, ready=None):
                for t in range(T):
                    dve.wait_ge(sem("filled_dve"), s.more("filled_dve"))
                    o = s.bank("dve")
                    tt(nat(dst, t), nat(dst, t), o[0:R, :], ALU.add).then_inc(sem(name), s.one(name))
                dve.wait_ge(*s.latest())
                if bias:
                    b = row(bias)
                    for t in range(T):
                        tt(nat(dst, t), nat(dst, t), b, ALU.add).then_inc(sem("dve_step"), s.one("dve_step"))
                    dve.wait_ge(*s.latest())
                    row_free(bias)

            dve.wait_ge(sem("edges_loaded"), s.more("edges_loaded", 32))
            for e in range(2):
                dve.tensor_copy(edges_f[e], edges_i[e]).then_inc(sem("edges_f"), s.one("edges_f"))
            dve.memset(ones[:, :], 1.0)
            dve.memset(proj[:, :, :], 0.0).then_inc(sem("proj_zero"), s.one("proj_zero"))
            dve.memset(EPS_LN, LN_EPS)
            dve.memset(EPS_PHI, 1e-4)
            dve.memset(EPS_RMS, 1e-6)
            dve.memset(sel[:, :, :], 0.0).then_inc(sem("dve_step"), s.one("dve_step"))
            dve.wait_ge(*s.latest())
            for c in range(KC):
                dve.memset(sel[0:64, c, 2 * c:2 * c + 1], 0.5 * float(DH) ** -0.5)
                ins = dve.memset(sel[64:128, c, 2 * c + 1:2 * c + 2], 0.5 * float(DH) ** -0.5)
            ins.then_inc(sem("dve_step"), s.one("dve_step"))
            dve.wait_ge(*s.latest())
            dve.memset(consts[:, 3:4], 0.0).then_inc(sem("consts_set"), s.one("consts_set"))
            dve.wait_ge(sem("iota"), s.more("iota", 1))
            dve.memset(zero16, 0.0).then_inc(sem("dve_step"), s.one("dve_step"))
            dve.wait_ge(*s.latest())
            dve.tensor_copy(iota16, iota_i).then_inc(sem("iota16"), s.one("iota16"))
            dve.wait_ge(sem("x_loaded"), s.more("x_loaded", 16))
            layer_norm(X, M, "xn")
            dve.wait_ge(sem("edgesT"), s.more("edgesT", 2))
            for dt in range(T):
                with dve.Fori(0, EC // EH_SLOTS) as it:
                    for j in range(EH_SLOTS):
                        dve.wait_ge(sem("onehot_used"), it * EH_SLOTS + (dt * EC + j + 1))
                        c = it * EH_SLOTS + j
                        ts(ohs[j][:, 0:N], iota16, edgesT[0][:, bass.ds(c, 1)], None, ALU.is_equal)
                        ts(ohd[j][:, 0:R], iota16[:, dt * R:(dt + 1) * R], edgesT[1][:, bass.ds(c, 1)], None,
                           ALU.is_equal).then_inc(sem("onehot"), 1)
            dve.wait_ge(sem("AT"), s.more("AT", 3 * T))
            dve.tensor_reduce(outdeg[0:R, :], AT[0:R, :].rearrange("p (s d) -> p s d", s=T), AX_X, ALU.add).then_inc(sem("dve_step"), s.one("dve_step"))
            dve.tensor_reduce(indeg[0:R, :], indeg3[0:R, :, :], AX_X, ALU.add).then_inc(sem("dve_step"), s.one("dve_step"))
            dve.wait_ge(*s.latest())
            ts(outdeg[0:R, :], outdeg[0:R, :], 1.0, None, ALU.add).then_inc(sem("degrees"), s.one("degrees"))
            ts(rcnt[0:R, :], indeg[0:R, :], 1.0, None, ALU.max).then_inc(sem("dve_step"), s.one("dve_step"))
            dve.wait_ge(*s.latest())
            dve.reciprocal(rcnt[0:R, :], rcnt[0:R, :]).then_inc(sem("dve_step"), s.one("dve_step"))
            dve.wait_ge(sem("deg_roots"), s.more("deg_roots", 2))
            dve.reciprocal(dis[0:R, :], dis[0:R, :]).then_inc(sem("dve_step"), s.one("dve_step"))
            dve.reciprocal(dinv[0:R, :], dinv[0:R, :]).then_inc(sem("dve_step"), s.one("dve_step"))
            dve.wait_ge(*s.latest())

            def scaled_rows(scale, bias):
                b = row(bias)
                for t in range(T):
                    dve.wait_ge(sem("filled_dve"), s.more("filled_dve"))
                    o = s.bank("dve")
                    tt(nat(Y, t), o[0:R, :], b, ALU.add).then_inc(sem("hs0"), s.one("hs0"))
                    dve.wait_ge(*s.latest())
                    ts(nat(Y, t), nat(Y, t), scale[0:R, t:t + 1], None, ALU.mult).then_inc(sem("hs"), s.one("hs"))
                row_free(bias)

            scaled_rows(dis, "L0gb")
            for t in range(T):
                dve.wait_ge(sem("filled_dve"), s.more("filled_dve"))
                o = s.bank("dve")
                v = tmp[0:R, t % 2, :]
                tt(v, o[0:R, :], nat(Y, t), ALU.add).then_inc(sem("gnn"), s.one("gnn"))
                dve.wait_ge(*s.latest())
                ts(v, v, dis[0:R, t:t + 1], 0.0, ALU.mult, ALU.max).then_inc(sem("dve_step"), s.one("dve_step"))
                dve.wait_ge(*s.latest())
                tt(nat(X, t), nat(X, t), v, ALU.add).then_inc(sem("dve_step"), s.one("dve_step"))

            dve.wait_ge(sem("proj_loaded"), s.more("proj_loaded", 64))
            ts(proj[:, :, :], proj[:, :, :], float(DH) ** -0.25, None, ALU.mult).then_inc(sem("proj_scaled"), s.one("proj_scaled"))

            def copy_diag():
                dve.wait_ge(sem("filled_dve"), s.more("filled_dve"))
                o = s.bank("dve")
                dve.tensor_copy(diag[0:R, :], o[0:R, 0:T * 8]).then_inc(sem("diag"), s.one("diag"))

            for dep in range(2):
                layer_norm(M, Y, "y")
                b = row(f"bv{dep}")
                for t in range(T):
                    dve.wait_ge(sem("filled_dve"), s.more("filled_dve"))
                    o = s.bank("dve")
                    vv = vaug(t, 0, HEADS).rearrange("p (h a) -> p h a", a=DA)
                    dve.memset(vv[:, :, DH:DA], 1.0)
                    tt(vv[:, :, 0:DH], o[0:R, :].rearrange("p (h a) -> p h a", a=DH),
                              b.rearrange("p (h a) -> p h a", a=DH), ALU.add).then_inc(sem("v"), s.one("v"))
                row_free(f"bv{dep}")
                copy_diag()
                for t in range(T):
                    for hp in range(4):
                        dve.wait_ge(sem("filled_dve"), s.more("filled_dve"))
                        o = s.bank("dve")
                        h = t * 8 + 2 * hp
                        dve.tensor_reduce(kmx[0:R, h:h + 2], o[0:R, :].rearrange("p (h m) -> p h m", h=2), AX_X, ALU.max).then_inc(sem("kmax"), s.one("kmax"))
                dve.wait_ge(*s.latest())
                dve.tensor_reduce(kh, kmx[0:R, :].rearrange("p (t h) -> p h t", h=8), AX_X, ALU.max).then_inc(sem("kh"), s.one("kh"))
                dve.wait_ge(sem("filled_dve"), s.more("filled_dve"))
                o = s.bank("dve")
                dve.tensor_reduce(km8, o[0:8, 0:R], AX_X, ALU.max).then_inc(sem("km8"), s.one("km8"))
                dve.wait_ge(*s.latest())
                ts(dg8, ident[0:8, 0:8], km8, None, ALU.mult).then_inc(sem("dg8"), s.one("dg8"))
                dve.wait_ge(sem("filled_dve"), s.more("filled_dve"))
                o = s.bank("dve")
                stt(nb[0:R, :].rearrange("p (t h) -> p t h", h=8), diag[0:R, :].rearrange("p (t h) -> p t h", h=8), -1.0,
                           o[0:R, 0:8].unsqueeze(1).to_broadcast([R, T, 8]), ALU.mult, ALU.subtract).then_inc(sem("knb"), s.one("knb"))
                for hp in range(4):
                    for t in range(T):
                        dve.wait_ge(sem("kp"), s.more("kp", 1))
                        sl = kp_slot[(hp * T + t) % 4]
                        ts(sl, sl, 1e-4, None, ALU.add).then_inc(sem("kpe"), s.one("kpe"))
                    dve.wait_ge(sem("filled_dve"), s.more("filled_dve"))
                    o = s.bank("dve")
                    dve.tensor_copy(ctxv[:, 2 * hp:2 * hp + 2, :, :].rearrange("p h m a -> p (h m a)"), o[:, 0:4 * DA]).then_inc(sem("ctx"), s.one("ctx"))
                copy_diag()
                dve.wait_ge(*s.latest())
                for i in range(T * 4 + 3):
                    if i < T * 4:
                        h = i // 4 * 8 + i % 4 * 2
                        dve.wait_ge(sem("filled_both"), s.more("filled_both"))
                        o = s.bank("both")
                        dve.tensor_reduce(kmx[0:R, h:h + 2], o[0:R, :].rearrange("p (h m) -> p h m", h=2), AX_X, ALU.max).then_inc(sem("dve_step"), s.one("dve_step"))
                        dve.wait_ge(*s.latest())
                        stt(nb[0:R, h:h + 2], diag[0:R, h:h + 2], -1.0, kmx[0:R, h:h + 2], ALU.mult, ALU.subtract).then_inc(sem("qmax"), s.one("qmax"))
                    if i >= 3:
                        t, hp = (i - 3) // 4, (i - 3) % 4
                        dve.wait_ge(sem("filled_dve"), s.more("filled_dve"))
                        o = s.bank("dve")
                        dve.reciprocal(rec2[i % 4], o[0:R, 0:2 * DA].rearrange("p (h a) -> p h a", a=DA)[:, :, DH]).then_inc(sem("dve_step"), s.one("dve_step"))
                        dve.wait_ge(*s.latest())
                        for h2 in range(2):
                            ins = ts(nat(YT, t, (2 * hp + h2) * DH, (2 * hp + h2 + 1) * DH), o[0:R, h2 * DA:h2 * DA + DH],
                                     rec2[i % 4][:, h2:h2 + 1], None, ALU.mult)
                        ins.then_inc(sem("o"), s.one("o"))
                add_to(M, "m_attn", f"bo{dep}")
                layer_norm(M, Y, "y")
                for b in range(4):
                    add_to(M, "m_ffn", f"b2{dep}" if b == 3 else None)
            for t in range(T):
                tt(nat(X, t), nat(X, t), nat(M, t), ALU.add).then_inc(sem("dve_step"), s.one("dve_step"))
            dve.wait_ge(*s.latest())

            for e in range(NE):
                ins = dve.memset(comb3[:, :, e:e + 1], 0.0)
            ins.then_inc(sem("dve_step"), s.one("dve_step"))
            rev = nb[0:R, :].rearrange("p (t e) -> p t e", e=NE)

            def bc(v):
                return v.unsqueeze(2).to_broadcast([R, T, NE])

            def gates(probs, pair_softmax, gbias=False):
                lg, w1, w2, s1, s2, vals2 = (small_k(i) for i in range(6))
                v1, v2, mr = diag[0:R, 0:T], diag[0:R, T:2 * T], diag[0:R, 2 * T:3 * T]

                def step(ins, name="dve_step"):
                    ins.then_inc(sem(name), s.one(name))
                    dve.wait_ge(*s.latest())
                for e in range(NE):
                    ins = dve.memset(rev[:, :, e:e + 1], float(NE - e))
                step(ins)
                dve.wait_ge(sem("filled_dve"), s.more("filled_dve"))
                o = s.bank("dve")
                step(dve.tensor_copy(lg, o[0:R, 0:T * 8].rearrange("p (t e) -> p t e", e=NE)), "logits")
                if gbias:
                    b = row("gb2")
                    step(tt(lg, lg, b[:, 0:NE].unsqueeze(1).to_broadcast([R, T, NE]), ALU.add))
                    row_free("gb2")
                if probs:
                    step(dve.tensor_reduce(mr, lg, AX_X, ALU.max))
                    step(tt(lg, lg, bc(mr), ALU.subtract), "gate_in0")
                    dve.wait_ge(sem("gate_exp0"), s.more("gate_exp0", 1))
                    step(dve.tensor_reduce(mr, lg, AX_X, ALU.add))
                    step(dve.reciprocal(mr, mr))
                    step(tt(lg, lg, bc(mr), ALU.mult))
                for vals, v, sel_ in ((lg, v1, s1), (vals2, v2, s2)):
                    step(dve.tensor_reduce(v, vals, AX_X, ALU.max))
                    step(tt(w1, vals, bc(v), ALU.is_equal))
                    step(tt(w1, w1, rev, ALU.mult))
                    step(dve.tensor_reduce(mr, w1, AX_X, ALU.max))
                    step(tt(sel_, w1, bc(mr), ALU.is_equal))
                    if vals is lg:
                        step(stt(vals2, s1, -BIG, lg, ALU.mult, ALU.add))
                if pair_softmax:
                    step(tt(GATE_D, v2, v1, ALU.subtract), "gate_in1")
                    dve.wait_ge(sem("gate_exp1"), s.more("gate_exp1", 1))
                    step(ts(mr, GATE_D, 1.0, None, ALU.add))
                    step(dve.reciprocal(v1, mr))
                    step(tt(v2, GATE_D, v1, ALU.mult))
                    step(tt(w1, s1, bc(v1), ALU.mult))
                    step(tt(w2, s2, bc(v2), ALU.mult))
                    step(tt(comb3, w1, w2, ALU.add), "comb")
                else:
                    step(tt(mr, v1, v2, ALU.add))
                    step(ts(mr, mr, 1e-20, None, ALU.add))
                    step(dve.reciprocal(mr, mr))
                    step(tt(w1, s1, s2, ALU.add))
                    step(tt(w1, w1, lg, ALU.mult))
                    step(tt(comb3, w1, bc(mr), ALU.mult), "comb")

            def expert_sum(e):
                for t in range(T):
                    dve.wait_ge(sem("filled_dve"), s.more("filled_dve"))
                    o = s.bank("dve")
                    stt(nat(X, t), o[0:R, :], comb[0:R, t * NE + e:t * NE + e + 1], nat(X, t), ALU.mult, ALU.add).then_inc(sem("moe"), s.one("moe"))

            layer_norm(X, Y, "y")
            gates(True, False)
            add_to(X, "moe_bias")
            row_free("E0")
            for e in range(NE):
                expert_sum(e)
                dve.wait_ge(*s.latest())
            add_to(X, "shared", "L0sb2")
            layer_norm(X, M, "xn")
            for t in range(T):
                dve.wait_ge(sem("filled_dve"), s.more("filled_dve"))
                o = s.bank("dve")
                ts(nat(Y, t), o[0:R, :], rcnt[0:R, t:t + 1], None, ALU.mult).then_inc(sem("agg"), s.one("agg"))
            dve.wait_ge(sem("bnT"), s.more("bnT", 12))
            for k in range(KC):
                for c, (t0, nt) in enumerate(CH):
                    ins = dve.bn_stats(stats[:, k * 3 + c, :], tr(Q, k, t0, nt))
            ins.then_inc(sem("dve_step"), s.one("dve_step"))
            dve.wait_ge(*s.latest())
            for k in range(KC):
                ins = dve.bn_aggr(mv[:, k, :], stats[:, 3 * k:3 * k + 3, :].rearrange("p a b -> p (a b)"))
            ins.then_inc(sem("bn_mv"), s.one("bn_mv"))
            dve.wait_ge(sem("std"), s.more("std", 1))
            dve.reciprocal(rstd[:, 0:KC], std[:, 0:KC]).then_inc(sem("dve_step"), s.one("dve_step"))
            dve.wait_ge(*s.latest())
            tt(colsT[:, 0:4], rstd[:, 0:KC], col("L1gamma", 0, 4), ALU.mult).then_inc(sem("dve_step"), s.one("dve_step"))
            dve.wait_ge(*s.latest())
            tt(rstd[:, 0:KC], mv[:, 0:KC, 0], colsT[:, 0:4], ALU.mult).then_inc(sem("dve_step"), s.one("dve_step"))
            dve.wait_ge(*s.latest())
            tt(colsT[:, 4:8], col("L1beta", 0, 4), rstd[:, 0:KC], ALU.subtract).then_inc(sem("bn_affine"), s.one("bn_affine"))
            for k in range(KC):
                dve.wait_ge(sem("bn_relu"), s.more("bn_relu", 1))
                for t0, nt in CH:
                    tt(tr(Q, k, t0, nt), tr(Q, k, t0, nt), tr(YT, k, t0, nt), ALU.add).then_inc(sem("bn_out"), s.one("bn_out"))
            add_to(X, "gnn")

            def linear_attention(layer):
                mem = layer == 1
                for t in range(T + 1):
                    if t < T:
                        dve.wait_ge(sem("filled_dve"), s.more("filled_dve"))
                        o = s.bank("dve")
                        o3 = o[0:R, :].rearrange("p (h c) -> p h c", c=DH)
                        mx = small[0:R, 16 * (t % 2):16 * (t % 2) + 8]
                        dve.tensor_reduce(mx, o3, AX_X, ALU.max).then_inc(sem("dve_step"), s.one("dve_step"))
                        dve.wait_ge(*s.latest())
                        tt(tmp[0:R, t % 2, :].rearrange("p (h c) -> p h c", c=DH), o3,
                                  mx.unsqueeze(2).to_broadcast([R, 8, DH]), ALU.subtract).then_inc(sem("qsub"), s.one("qsub"))
                    if t >= 1:
                        dve.wait_ge(sem("qexp"), s.more("qexp", 1))
                        sm = small[0:R, 8 + 16 * (t % 2):16 + 16 * (t % 2)]
                        v = tmp[0:R, (t - 1) % 2, :].rearrange("p (h c) -> p h c", c=DH)
                        dve.tensor_reduce(sm, v, AX_X, ALU.add).then_inc(sem("dve_step"), s.one("dve_step"))
                        dve.wait_ge(*s.latest())
                        dve.reciprocal(sm, sm).then_inc(sem("dve_step"), s.one("dve_step"))
                        dve.wait_ge(*s.latest())
                        if mem:
                            ts(sm, sm, float(DH) ** -0.5, None, ALU.mult).then_inc(sem("dve_step"), s.one("dve_step"))
                            dve.wait_ge(*s.latest())
                        tt(nat(Y, t - 1).rearrange("p (h c) -> p h c", c=DH), v,
                                  sm.unsqueeze(2).to_broadcast([R, 8, DH]), ALU.mult).then_inc(sem("qn"), s.one("qn"))
                if mem:
                    dve.memset(small[0:R, 0:1], 0.0).then_inc(sem("qn_last"), s.one("qn_last"))
                for k in range(KC):
                    dve.wait_ge(sem("kT2"), s.more("kT2", 3))
                    dve.tensor_reduce(small[:, 8 + k:9 + k], K[:, k * N:(k + 1) * N], AX_X, ALU.max).then_inc(sem("dve_step"), s.one("dve_step"))
                    if mem:
                        dve.tensor_reduce(small[:, 12 + k:13 + k], col("memk", 8 * k, 8), AX_X, ALU.max).then_inc(sem("dve_step"), s.one("dve_step"))
                        dve.wait_ge(*s.latest())
                        tt(small[:, 8 + k:9 + k], small[:, 8 + k:9 + k], small[:, 12 + k:13 + k], ALU.max).then_inc(sem("dve_step"), s.one("dve_step"))
                    dve.wait_ge(*s.latest())
                    ts(kneg[:, k:k + 1], small[:, 8 + k:9 + k], -1.0, None, ALU.mult).then_inc(sem("k_max"), s.one("k_max"))
                for t in range(T):
                    dve.wait_ge(sem("filled_dve"), s.more("filled_dve"))
                    o = s.bank("dve")
                    dve.tensor_copy(nat(M, t), o[0:R, :]).then_inc(sem("v2"), s.one("v2"))
                dve.wait_ge(sem("kexp"), s.more("kexp", 1))
                if mem:
                    tt(ksum, ksum, ksum2, ALU.add).then_inc(sem("dve_step"), s.one("dve_step"))
                    dve.wait_ge(*s.latest())
                dve.reciprocal(small[:, 8:12], ksum).then_inc(sem("dve_step"), s.one("dve_step"))
                dve.wait_ge(sem("kn"), s.more("kn", T))
                for hp in range(4):
                    dve.wait_ge(sem("filled_dve"), s.more("filled_dve"))
                    o = s.bank("dve")
                    if hp == 0:
                        dve.wait_ge(*s.latest())
                    dve.memset(bd[:, hp * 128:(hp + 1) * 128], 0.0).then_inc(sem("dve_step"), s.one("dve_step"))
                    dve.wait_ge(*s.latest())
                    ts(bd[0:64, hp * 128:hp * 128 + 64], o[0:64, 0:64], small[0:64, 8 + hp:9 + hp], None, ALU.mult)
                    ts(bd[64:128, hp * 128 + 64:hp * 128 + 128], o[64:128, 64:128], small[64:128, 8 + hp:9 + hp], None, ALU.mult).then_inc(sem("ctx2"), s.one("ctx2"))
                b = row("L1bout" if mem else "L2bout")
                for t in range(T):
                    dve.wait_ge(sem("filled_dve"), s.more("filled_dve"))
                    o = s.bank("dve")
                    if mem:
                        tt(nat(Y, t), o[0:R, :], b, ALU.add).then_inc(sem("att_out"), s.one("att_out"))
                    else:
                        v = tmp[0:R, t % 2, :]
                        tt(v, o[0:R, :], b, ALU.add).then_inc(sem("att_out"), s.one("att_out"))
                        dve.wait_ge(*s.latest())
                        tt(nat(X, t), nat(X, t), v, ALU.add).then_inc(sem("dve_step"), s.one("dve_step"))
                dve.wait_ge(*s.latest())
                row_free("L1bout" if mem else "L2bout")
                if mem:
                    dve.wait_ge(sem("std"), s.more("std", 1))
                    inverse_norms()
                    b = row("L1onw")
                    for t in range(T):
                        stt(nat(Y, t), nat(Y, t), rstd[0:R, t:t + 1], b, ALU.mult, ALU.mult).then_inc(sem("dve_step"), s.one("dve_step"))
                    dve.wait_ge(*s.latest())
                    row_free("L1onw")
                    for t in range(T):
                        stt(nat(X, t), nat(Y, t), float(D) ** 0.5, nat(X, t), ALU.mult, ALU.add).then_inc(sem("dve_step"), s.one("dve_step"))
                    dve.wait_ge(*s.latest())

            def inverse_norms():
                ts(std[0:R, :], std[0:R, :], 1e-12, None, ALU.max).then_inc(sem("dve_step"), s.one("dve_step"))
                dve.wait_ge(*s.latest())
                dve.reciprocal(rstd[0:R, :], std[0:R, :]).then_inc(sem("dve_step"), s.one("dve_step"))
                dve.wait_ge(*s.latest())

            dve.memset(small[0:R, 0:1], 0.0).then_inc(sem("xn_all"), s.one("xn_all"))
            ts(col("L1nw", 0, 4), col("L1nw", 0, 4), float(D) ** 0.5, None, ALU.mult).then_inc(sem("nw_scaled"), s.one("nw_scaled"))
            dve.wait_ge(sem("std"), s.more("std", 1))
            inverse_norms()
            for t in range(T):
                ts(nat(Y, t), nat(M, t), rstd[0:R, t:t + 1], None, ALU.mult).then_inc(sem("y"), s.one("y"))
            linear_attention(1)
            layer_norm(X, Y, "y")
            gates(True, True, gbias=True)
            add_to(X, "moe_bias")
            row_free("E1")
            for b in range(2 * NE):
                expert_sum(b // 2)
                dve.wait_ge(*s.latest())
            layer_norm(X, M, "xn")
            for k in range(KC):
                for t0, nt in CH:
                    dve.wait_ge(sem("filled_dve"), s.more("filled_dve"))
                    o = s.bank("dve")
                    tt(tr(K, k, t0, nt), o[:, 0:nt * R], tr(YT, k, t0, nt), ALU.add).then_inc(sem("gT"), s.one("gT"))
            add_to(X, "gnn", "L2gb2")
            linear_attention(2)
            layer_norm(X, Y, "y")
            gates(False, True)
            for pair in range(NE // 2):
                for half in range(2):
                    for k in range(KC):
                        dve.wait_ge(sem("g1T"), s.more("g1T", 3))
                        tt(M[:, k * N:(k + 1) * N], Q[:, k * N:(k + 1) * N], Q[:, k * N:(k + 1) * N], ALU.mult).then_inc(sem("sqT"), s.one("sqT"))
                    for e in range(2):
                        dve.wait_ge(sem("rms"), s.more("rms", 3))
                        dve.reciprocal(Y[:, e * N:(e + 1) * N], Y[:, e * N:(e + 1) * N]).then_inc(sem("dve_step"), s.one("dve_step"))
                    dve.wait_ge(*s.latest())
                    for k in range(KC):
                        e = k // 2
                        sc = col("L2n1" if half == 0 else "L2n2", (2 * pair + e) * 2 + k % 2)
                        dst = K if half == 0 else Q
                        ins = stt(dst[:, k * N:(k + 1) * N], Q[:, k * N:(k + 1) * N], sc, Y[:, e * N:(e + 1) * N], ALU.mult, ALU.mult)
                        if half == 0:
                            ins.then_inc(sem("h1"), s.one("h1"))
                        else:
                            ins.then_inc(sem("dve_step"), s.one("dve_step"))
                            dve.wait_ge(*s.latest())
                            tt(K[:, k * N:(k + 1) * N], K[:, k * N:(k + 1) * N], Q[:, k * N:(k + 1) * N], ALU.add).then_inc(sem("h12"), s.one("h12"))
                    dve.wait_ge(*s.latest())
                for e in range(2):
                    expert_sum(2 * pair + e)
                    dve.wait_ge(*s.latest())
            layer_norm(X, M, "xn")
            for t in range(T):
                dve.wait_ge(sem("filled_dve"), s.more("filled_dve"))
                o = s.bank("dve")
                ts(nat(Y, t), o[0:R, :], dinv[0:R, t:t + 1], None, ALU.mult).then_inc(sem("hs3"), s.one("hs3"))
            dve.wait_ge(*s.latest())
            b = row("L3gb")
            for t in range(T):
                dve.wait_ge(sem("filled_dve"), s.more("filled_dve"))
                o = s.bank("dve")
                v = tmp[0:R, t % 2, :]
                tt(v, o[0:R, :], nat(Y, t), ALU.add).then_inc(sem("gnn"), s.one("gnn"))
                dve.wait_ge(*s.latest())
                stt(v, v, dinv[0:R, t:t + 1], b, ALU.mult, ALU.add).then_inc(sem("dve_step"), s.one("dve_step"))
                dve.wait_ge(*s.latest())
                stt(v, v, 0.01, v, ALU.mult, ALU.max).then_inc(sem("dve_step"), s.one("dve_step"))
                dve.wait_ge(*s.latest())
                tt(nat(X, t), nat(X, t), v, ALU.add).then_inc(sem("dve_step"), s.one("dve_step"))
            dve.wait_ge(*s.latest())
            row_free("L3gb")
            dve.memset(small[0:1, 0:1], 0.0).then_inc(sem("gnn_read"), s.one("gnn_read"))
            dve.wait_ge(sem("filled_dve"), s.more("filled_dve"))
            o = s.bank("dve")
            ts(colsT[:, 0:4], o[:, 0:4], 1.0 / N, None, ALU.mult).then_inc(sem("colsum"), s.one("colsum"))
            dve.wait_ge(*s.latest())
            for k in range(KC):
                ins = ts(tmp[:, 0, k * R:(k + 1) * R], ones[:, 0:R], colsT[:, k:k + 1], None, ALU.mult)
            ins.then_inc(sem("mean_bc"), s.one("mean_bc"))
            dve.wait_ge(sem("filled_dve"), s.more("filled_dve"))
            o = s.bank("dve")
            dve.tensor_copy(tmp[0:R, 1, :], o[0:R, :]).then_inc(sem("first"), s.one("first"))
            dve.wait_ge(*s.latest())
            for t in range(T):
                dve.wait_ge(sem("filled_dve"), s.more("filled_dve"))
                o = s.bank("dve")
                tt(nat(X, t), nat(X, t), o[0:R, :], ALU.add).then_inc(sem("x_mix"), s.one("x_mix"))
                dve.wait_ge(*s.latest())
                tt(nat(X, t), nat(X, t), tmp[0:R, 1, :], ALU.add).then_inc(sem("dve_step"), s.one("dve_step"))
            dve.wait_ge(*s.latest())
            layer_norm(X, Y, "y")
            gates(False, True)
            add_to(X, "moe_bias")
            row_free("E2")
            for e in range(NE):
                expert_sum(e)
                dve.wait_ge(*s.latest())
            dve.memset(small[0:1, 0:1], 0.0).then_inc(sem("result"), s.one("result"))

        @block.gpsimd
        def _(pool):
            pool.memset(ident[:, :], 0.0).then_inc(sem("pool_step"), 1)
            pool.wait_ge(sem("pool_step"), 1)
            pool.affine_select(out=ident[:, :], in_=ident[:, :], compare_op=ALU.not_equal, fill=1.0, base=0,
                               pattern=[[-1, 128]], channel_multiplier=1).then_inc(sem("ident"), 1)
            pool.iota(iota_i, pattern=[[1, N]], base=0, channel_multiplier=0).then_inc(sem("iota"), 1)
            for j, name in enumerate(ROWS):
                if j:
                    pool.wait_ge(sem(row_release[j - 1][0]), row_release[j - 1][1])
                if name[0] == "E":
                    pool.dma_start(row_slot[0:NE, :], eb_in[int(name[1])]).then_inc(sem("row_loaded"), 16)
                elif name == "gb2":
                    pool.dma_start(row_slot[0:R, 0:NE], gb2_in.partition_broadcast(R)).then_inc(sem("row_loaded"), 16)
                else:
                    pool.dma_start(row_slot[0:R, :], rows_in[VEC_ROWS.index(name), :].partition_broadcast(R)).then_inc(sem("row_loaded"), 16)

        @block.sync
        def _(sp):
            sp.dma_start(edges_i[0], src_in.rearrange("(r c) -> r c", r=EROWS)).then_inc(sem("edges_loaded"), 16)
            sp.dma_start(edges_i[1], dst_in.rearrange("(r c) -> r c", r=EROWS)).then_inc(sem("edges_loaded"), 16)
            sp.dma_start(X[0:R, :].rearrange("p (t d) -> p t d", t=T), x_in.rearrange("(t p) d -> p t d", p=R)).then_inc(sem("x_loaded"), 16)
            sp.dma_start(cols[:, :], cols_in[:, :]).then_inc(sem("cols_loaded"), 16)
            sp.wait_ge(sem("proj_zero"), 1)
            for dep in range(2):
                for h2 in range(2):
                    sp.dma_start(proj[h2 * DH:(h2 + 1) * DH, dep, h2 * NBF:(h2 + 1) * NBF],
                                 proj_in[dep]).then_inc(sem("proj_loaded"), 16)
            for u in range(N_UNITS):
                if u >= UNIT_SLOTS:
                    name, value = unit_release[u - UNIT_SLOTS]
                    sp.wait_ge(sem(name), value)
                sp.dma_start(units[:, u % UNIT_SLOTS, :], units_in[u]).then_inc(sem(f"unit_loaded{u % UNIT_SLOTS}"), 16)
            sp.wait_ge(sem("result"), 1)
            sp.dma_start(out.rearrange("(t p) d -> p t d", p=R), X[0:R, :].rearrange("p (t d) -> p t d", t=T)).then_inc(sem("out_stored"), 16)
            sp.wait_ge(sem("out_stored"), 16)


def _layout(a):
    import numpy as np

    def unit(w):
        return w.reshape(KC, 128, D).transpose(1, 0, 2).reshape(128, KC * D)

    u = [a["L0_gnn_W"].T]
    for i in range(2):
        u += [a["L0_mix_Wk"][i], a["L0_mix_Wv"][i], a["L0_mix_Wq"][i], a["L0_mix_Wo"][i]]
        for b in range(4):
            u += [a["L0_mix_W1"][i][:, b * D:(b + 1) * D], a["L0_mix_W2"][i][b * D:(b + 1) * D]]
    for b in range(2):
        u += [np.concatenate(list(a["L0_ffn_w1"][4 * b:4 * b + 4]), 1), a["L0_ffn_w2"][4 * b:4 * b + 4].reshape(D, D)]
    u += [a["L0_ffn_sw1"], a["L0_ffn_sw2"], a["L1_gnn_W_l"].T, a["L1_gnn_W_r"].T]
    u += [a["L1_mix_w_qkv"][:, i * D:(i + 1) * D] for i in range(3)] + [a["L1_mix_w_out"]]
    u += [np.concatenate([a["L1_ffn_gw1"]] * 2, 1)]
    for e in range(NE):
        for b in range(2):
            u += [a["L1_ffn_we1"][e][:, b * D:(b + 1) * D], a["L1_ffn_we2"][e][b * D:(b + 1) * D]]
    u += [a["L2_gnn_W1"], a["L2_gnn_W2"]]
    u += [a["L2_mix_Wqkv"][i * D:(i + 1) * D].T for i in range(3)] + [a["L2_mix_Wout"].T]
    units = [unit(w) for w in u]
    for p in range(4):
        units += [unit(np.concatenate(list(a["L2_ffn_w1"][2 * p:2 * p + 2]), 1))]
        if p % 2 == 0:
            units += [a["L2_ffn_w2"][2 * p:2 * p + 4].reshape(8, 128, 256).transpose(1, 0, 2).reshape(128, KC * D)]
        units += [unit(a["L2_ffn_w3"][2 * p:2 * p + 2].reshape(D, D))]
    u = [a["L3_gnn_W"], a["L3_mix_W_v"].T, a["L3_mix_W_theta"].T]
    for p in range(4):
        u += [np.concatenate(list(a["L3_ffn_w1"][2 * p:2 * p + 2]), 1), a["L3_ffn_w2"][2 * p:2 * p + 2].reshape(D, D)]
    units = np.stack(units + [unit(w) for w in u])

    def vec(v):
        return v.reshape(-1, 128).T

    def gate(w):
        return w.reshape(-1, 128, NE).transpose(1, 0, 2).reshape(128, -1)

    c = {}
    for i in range(2):
        for n, s in (("ln1g", "ln1_g"), ("ln1b", "ln1_b"), ("ln2g", "ln2_g"), ("ln2b", "ln2_b"), ("bq", "bq"), ("bk", "bk"), ("b1", "b1")):
            c[f"L0{n}{i}"] = vec(a[f"L0_mix_{s}"][i])
    for n, s in (("L0eb1", "L0_ffn_b1"), ("L0sb1", "L0_ffn_sb1"), ("L1bl", "L1_gnn_b_l"), ("L1gamma", "L1_gnn_gamma"),
                 ("L1beta", "L1_gnn_beta"), ("L1nw", "L1_mix_norm_w"), ("L1gb1", "L1_ffn_gb1"), ("L1be1", "L1_ffn_be1"),
                 ("L2b1", "L2_gnn_b1"), ("L2n1", "L2_ffn_n1"), ("L2n2", "L2_ffn_n2"), ("L3eb1", "L3_ffn_b1")):
        c[n] = vec(a[s].reshape(-1))
    c["L0gate"] = gate(a["L0_ffn_gate_w"].T)
    c["L1gate"] = gate(a["L1_ffn_gw2"])
    c["L2gate"] = gate(a["L2_ffn_gate_w"])
    c["L3gate"] = gate(a["L3_ffn_gate_w"].T)
    c["memk"] = gate(a["L1_mix_mem_kv"][0].reshape(D, NE))
    c["memv"] = gate(a["L1_mix_mem_kv"][1].reshape(D, NE))
    cols = np.concatenate([c[n] for n in COLS], 1)
    r = {"L0gb": a["L0_gnn_b"], "L0sb2": a["L0_ffn_sb2"], "L1bout": a["L1_mix_b_out"], "L1onw": a["L1_mix_out_norm_w"].reshape(-1),
         "L2gb2": a["L2_gnn_b2"], "L2bout": a["L2_mix_bout"], "L3gb": a["L3_gnn_b"]}
    for i in range(2):
        r[f"bv{i}"], r[f"bo{i}"], r[f"b2{i}"] = a["L0_mix_bv"][i], a["L0_mix_bo"][i], a["L0_mix_b2"][i]
    rows = np.stack([r[n] for n in VEC_ROWS])
    eb = np.stack([a["L0_ffn_b2"], a["L1_ffn_be2"], a["L3_ffn_b2"]])
    proj = a["L0_mix_proj"].transpose(0, 2, 1)
    return {"x": a["x"], "src": a["src"], "dst": a["dst"], "units": units, "cols": cols, "rows": rows, "eb": eb,
            "gb2": a["L1_ffn_gb2"], "proj": proj}


def kernel(**inputs):
    import numpy as np
    import concourse.bacc as bacc
    from concourse.bass_utils import run_bass_kernel_spmd

    nc = bacc.Bacc("TRN2", target_bir_lowering=False, num_devices=1)
    arrays, args = {}, []
    for name, a in _layout({n: np.asarray(v) for n, v in inputs.items()}).items():
        a = np.ascontiguousarray(a)
        arrays[f"in_{name}"] = a
        args.append(nc.dram_tensor(f"in_{name}", a.shape, mybir.dt.from_np(a.dtype), kind="ExternalInput").ap())
    args.append(nc.dram_tensor("out_0", (N, D), F32, kind="ExternalOutput").ap())
    build(nc, *args)
    r = run_bass_kernel_spmd(nc, [arrays], core_ids=[0])
    return r.results[0]["out_0"]
```
